# Optimizing a Trainium2 kernel written in Bass

```python
import numpy as np
import jax
import jax.numpy as jnp

def _softmax(x, axis=-1):
    return jax.nn.softmax(x, axis=axis)

def _gelu(x):
    return jax.nn.gelu(x, approximate=True)

def _silu(x):
    return jax.nn.silu(x)

def _sigmoid(x):
    return jax.nn.sigmoid(x)

def _layernorm(x, axis=-1, eps=1e-05):
    m = jnp.mean(x, axis=axis, keepdims=True)
    v = jnp.var(x, axis=axis, keepdims=True)
    return (x - m) / jnp.sqrt(v + eps)

def _scatter_add(tgt, idx, src, axis=0):
    return tgt.at[idx].add(src)

def _segment_sum(src, seg, n):
    return jax.ops.segment_sum(src, seg, n)
kernel_name = 'mk_conv_attn_hybrid_d2_conv_nhwc512_r2_369eb1'

def setup_inputs(seed: int=0):
    np.random.seed(seed)
    _w = jnp.asarray

    def _rec_inputs():
        import jax
        import jax.numpy as jnp
        _gk = jax.random.key(seed)
        x = -0.0003929 + 0.9999 * jax.random.normal(jax.random.fold_in(_gk, 1), (8, 32, 32, 256), jnp.float32)
        return x
    x = _rec_inputs()

    def _L0_conv_setup():
        import jax, jax.numpy as jnp
        import numpy as np
        HEADS = 8
        DIM_HEAD = 32
        LN_EPS = 1e-05

        def _layernorm(x, gamma, beta):
            mu = jnp.mean(x, axis=-1, keepdims=True)
            var = jnp.mean(jnp.square(x - mu), axis=-1, keepdims=True)
            return (x - mu) * jax.lax.rsqrt(var + LN_EPS) * gamma + beta
        key = jax.random.key(seed)
        k1, k2 = jax.random.split(key)
        B, L, W, C = (8, 32, 32, 256)
        inner = HEADS * DIM_HEAD
        x = jax.random.normal(k1, (B, L, W, C), dtype=jnp.float32)
        w_qkv = jax.random.normal(k2, (C, 3 * inner), dtype=jnp.float32) * 0.02
        q_gamma = jnp.ones((DIM_HEAD,), dtype=jnp.float32)
        q_beta = jnp.zeros((DIM_HEAD,), dtype=jnp.float32)
        k_gamma = jnp.ones((DIM_HEAD,), dtype=jnp.float32)
        k_beta = jnp.zeros((DIM_HEAD,), dtype=jnp.float32)
        return {'x': x, 'w_qkv': w_qkv, 'q_gamma': q_gamma, 'q_beta': q_beta, 'k_gamma': k_gamma, 'k_beta': k_beta}
    _L0_conv_all = _L0_conv_setup()
    _L0_conv_in = {k: v for k, v in _L0_conv_all.items() if k in ('w_qkv', 'q_gamma', 'q_beta', 'k_gamma', 'k_beta')}
    del _L0_conv_all

    def _L1_attn_setup():
        import jax, jax.numpy as jnp
        import numpy as np
        from math import sqrt
        key = jax.random.key(seed)
        k1, k2, k3, k4 = jax.random.split(key, 4)
        bs, N, D, H = (2, 2048, 256, 8)
        z = jax.random.normal(k1, (bs, N, D), dtype=jnp.float32)
        w_qkv = jax.random.normal(k2, (3 * D, D), dtype=jnp.float32) * (1.0 / sqrt(D))
        w_agg = jax.random.normal(k3, (D, D), dtype=jnp.float32) * (1.0 / sqrt(D))
        b_agg = jax.random.normal(k4, (D,), dtype=jnp.float32) * 0.01
        return {'z': z, 'w_qkv': w_qkv, 'w_agg': w_agg, 'b_agg': b_agg}
    _L1_attn_all = _L1_attn_setup()
    _L1_attn_in = {k: v for k, v in _L1_attn_all.items() if k in ('w_qkv', 'w_agg', 'b_agg')}
    del _L1_attn_all

    def _L1_ffn_setup():
        import jax, jax.numpy as jnp
        import numpy as np
        EPS = 1e-06
        SINKHORN_ITERS = 8
        TEMPERATURE = 1.0
        B, N, D = (4, 4096, 256)
        E, OUT = (8, 256)
        H = 1

        def _sinkhorn(logits):
            t = jnp.log(jnp.clip(logits, EPS)) / TEMPERATURE
            for _ in range(SINKHORN_ITERS):
                t = t - jax.nn.logsumexp(t, axis=-2, keepdims=True)
                t = t - jax.nn.logsumexp(t, axis=-1, keepdims=True)
            return jnp.exp(t)
        key = jax.random.key(seed)
        k1, k2, k3 = jax.random.split(key, 3)
        x = jax.random.normal(k1, (B, N, D), dtype=jnp.float32)
        gate_weight = jax.random.normal(k2, (H, D, E), dtype=jnp.float32)
        experts = jax.random.normal(k3, (E, D, OUT), dtype=jnp.float32) * 0.02
        return {'x': x, 'gate_weight': gate_weight, 'experts': experts}
    _L1_ffn_all = _L1_ffn_setup()
    _L1_ffn_in = {k: v for k, v in _L1_ffn_all.items() if k in ('gate_weight', 'experts')}
    del _L1_ffn_all
    return {'x': x, 'L0_conv_w_qkv': _L0_conv_in['w_qkv'], 'L0_conv_q_gamma': _L0_conv_in['q_gamma'], 'L0_conv_q_beta': _L0_conv_in['q_beta'], 'L0_conv_k_gamma': _L0_conv_in['k_gamma'], 'L0_conv_k_beta': _L0_conv_in['k_beta'], 'L1_attn_w_qkv': _L1_attn_in['w_qkv'], 'L1_attn_w_agg': _L1_attn_in['w_agg'], 'L1_attn_b_agg': _L1_attn_in['b_agg'], 'L1_ffn_gate_weight': _L1_ffn_in['gate_weight'], 'L1_ffn_experts': _L1_ffn_in['experts']}

def reference(x, L0_conv_w_qkv, L0_conv_q_gamma, L0_conv_q_beta, L0_conv_k_gamma, L0_conv_k_beta, L1_attn_w_qkv, L1_attn_w_agg, L1_attn_b_agg, L1_ffn_gate_weight, L1_ffn_experts):
    import jax
    import jax.numpy as jnp

    def _L0_conv_ref(x, w_qkv, q_gamma, q_beta, k_gamma, k_beta):
        import jax, jax.numpy as jnp
        import numpy as np
        HEADS = 8
        DIM_HEAD = 32
        LN_EPS = 1e-05

        def _layernorm(x, gamma, beta):
            mu = jnp.mean(x, axis=-1, keepdims=True)
            var = jnp.mean(jnp.square(x - mu), axis=-1, keepdims=True)
            return (x - mu) * jax.lax.rsqrt(var + LN_EPS) * gamma + beta
        B, L, W, C = x.shape
        n = L * W
        xf = x.reshape(B, n, C)
        qkv = xf @ w_qkv
        q, k, v = jnp.split(qkv, 3, axis=-1)

        def to_heads(t):
            return t.reshape(B, n, HEADS, DIM_HEAD).transpose(0, 2, 1, 3)
        q, k, v = (to_heads(q), to_heads(k), to_heads(v))
        q = _layernorm(q, q_gamma, q_beta)
        k = _layernorm(k, k_gamma, k_beta)
        dots = jnp.einsum('bhnd,bhne->bhde', k, v)
        out = jnp.einsum('bhnd,bhde->bhne', q, dots) * (1.0 / n)
        out = out.transpose(0, 2, 1, 3).reshape(B, L, W, HEADS * DIM_HEAD)
        return out

    def _L1_attn_ref(z, w_qkv, w_agg, b_agg):
        import jax, jax.numpy as jnp
        import numpy as np
        from math import sqrt
        bs, N, D = z.shape
        H = 8
        Dh = D // H
        qkv = jnp.einsum('bnd,ed->bne', z, w_qkv).reshape(bs, N, 3, H, Dh)
        q, k, v = jnp.moveaxis(qkv, 2, 0)
        q = q.transpose(0, 2, 1, 3)
        k = k.transpose(0, 2, 1, 3)
        v = v.transpose(0, 2, 1, 3)
        scores = jnp.einsum('bhnd,bhmd->bhnm', q, k) / sqrt(Dh)
        attn = jax.nn.softmax(scores, axis=-1)
        sa = jnp.einsum('bhnm,bhmd->bhnd', attn, v)
        sa = sa.transpose(0, 2, 1, 3).reshape(bs, N, H * Dh)
        out = jnp.einsum('bnd,ed->bne', sa, w_agg) + b_agg
        return out

    def _L1_ffn_ref(x, gate_weight, experts):
        import jax, jax.numpy as jnp
        import numpy as np
        EPS = 1e-06
        SINKHORN_ITERS = 8
        TEMPERATURE = 1.0
        B, N, D = (4, 4096, 256)
        E, OUT = (8, 256)
        H = 1

        def _sinkhorn(logits):
            t = jnp.log(jnp.clip(logits, EPS)) / TEMPERATURE
            for _ in range(SINKHORN_ITERS):
                t = t - jax.nn.logsumexp(t, axis=-2, keepdims=True)
                t = t - jax.nn.logsumexp(t, axis=-1, keepdims=True)
            return jnp.exp(t)
        b, n, d = x.shape
        e = experts.shape[0]
        m = n // e
        xh = x[:, None, :, :]
        gate_logits = jnp.einsum('bhnd,hde->bhne', xh, gate_weight)
        gates = _sinkhorn(gate_logits)
        g_t = jnp.swapaxes(gates, -1, -2)
        vals, idx = jax.lax.top_k(g_t, m)
        gate_values = jnp.transpose(vals, (2, 0, 1, 3))[..., None]
        routed = jnp.take_along_axis(xh[:, :, None, :, :], idx[..., None], axis=3)
        routed = jnp.transpose(routed, (2, 0, 1, 3, 4))
        expert_w = experts[:, None, :, :]
        outputs = jnp.einsum('ebhmi,ehio->ebhmo', routed, expert_w)
        outputs = outputs * gate_values
        bh_idx = idx.reshape(b, 1, e * m)
        bh_vals = jnp.transpose(outputs, (1, 2, 0, 3, 4)).reshape(b, 1, e * m, outputs.shape[-1])

        def scat(i1, v1):
            return jnp.zeros((n, v1.shape[-1]), dtype=v1.dtype).at[i1].set(v1)
        routed_back = jax.vmap(jax.vmap(scat))(bh_idx, bh_vals)
        return routed_back[:, 0]

    def _gn(v, G=32, eps=1e-05):
        B_, H_, W_, C_ = v.shape
        g = v.reshape(B_, H_, W_, G, C_ // G)
        m = jnp.mean(g, axis=(1, 2, 4), keepdims=True)
        s = jnp.var(g, axis=(1, 2, 4), keepdims=True)
        return ((g - m) / jnp.sqrt(s + eps)).reshape(v.shape)

    def _ln_c(v, eps=1e-06):
        m = jnp.mean(v, axis=-1, keepdims=True)
        s = jnp.var(v, axis=-1, keepdims=True)
        return (v - m) / jnp.sqrt(s + eps)

    def _ln_t(v, eps=1e-05):
        m = jnp.mean(v, axis=-1, keepdims=True)
        s = jnp.var(v, axis=-1, keepdims=True)
        return (v - m) / jnp.sqrt(s + eps)

    def _to_tokens(v):
        B_, H_, W_, C_ = v.shape
        return v.reshape(B_, H_ * W_, C_)

    def _from_tokens(t, like):
        return t.reshape(like.shape)
    x = x + _L0_conv_ref(_gn(x), L0_conv_w_qkv, L0_conv_q_gamma, L0_conv_q_beta, L0_conv_k_gamma, L0_conv_k_beta)
    t = _to_tokens(x)
    t = t + _L1_attn_ref(_ln_t(t), L1_attn_w_qkv, L1_attn_w_agg, L1_attn_b_agg)
    t = t + _L1_ffn_ref(_ln_t(t), L1_ffn_gate_weight, L1_ffn_experts)
    x = _from_tokens(t, x)
    return x

_drawn_inputs = setup_inputs


def setup_inputs(seed=0):
    import zlib

    import numpy as np

    out = dict(_drawn_inputs(seed))
    spreads = {'L0_conv_q_gamma': (1.0, 0.2),
     'L0_conv_q_beta': (0.0, 0.33),
     'L0_conv_k_gamma': (1.0, 0.2),
     'L0_conv_k_beta': (0.0, 0.569)}
    factors = {'L1_attn_b_agg': 4.233}
    for name, (base, spread) in spreads.items():
        noise = np.random.default_rng([zlib.crc32(name.encode()), seed]).standard_normal(out[name].shape)
        drawn = base * np.exp(spread * noise) if base else spread * noise
        out[name] = jnp.asarray(drawn.astype(out[name].dtype))
    for name, factor in factors.items():
        out[name] = (out[name] * factor).astype(out[name].dtype)
    return out
```

```python
import numpy as np
import concourse.bass as bass
from concourse import mybir
from contextlib import ExitStack

F32 = mybir.dt.float32
F32R = mybir.dt.float32r
I32 = mybir.dt.int32
U32 = mybir.dt.uint32
ALU = mybir.AluOpType
ACT = mybir.ActivationFunctionType
AX = mybir.AxisListType

P = 128
B = 8
N = 1024
C = 256
T = N // P
CH = C // P
H = 8
DH = C // H
HG = P // DH
G = H // HG
E = 8
M = N // E
GROUP = C // 32
BANK = 512
QB = 256
NQB = N // QB
BLOCK_UNITS = T
UNITS = G * NQB * BLOCK_UNITS
SINKHORN_ITERS = 8
LN_EPS = 1e-5
CLIP = 1e-6
MAX_ROW = 3 * DH
RSQRT_SEED = 0x5F3759DF


def merged(main, extra, lead=1.15):
    out, j = [], 0
    for i, s in enumerate(main):
        out.append(s)
        while j < len(extra) and j * len(main) < (i + 1) * len(extra) * lead:
            out.append(extra[j])
            j += 1
    return out


def spread(steps, slots):
    return [steps[len(steps) * u // slots:len(steps) * (u + 1) // slots] for u in range(slots)]


STORE = [("agg", t) for t in range(T)] + [("store_stats",)] + [("z2T", t) for t in range(T)] + [("gate",)]
FRONT_A = ([("xT", c, h) for c in range(CH) for h in range(2)] + [("gmean",), ("gvar",)]
           + [(k, t) for t in range(T // 2) for k in ("qk0", "v0")] + [("head_scale", 0)]
           + [(k, t) for t in range(T // 2, T) for k in ("qk0", "v0")] + [("head_scale", 1)]
           + [("sumv",), ("dots",)] + [("qT", c, h) for c in range(CH) for h in range(2)]
           + [("lin", t) for t in range(T)] + [("front_stats",)]
           + [("zT", c, h) for c in range(CH) for h in range(2)]
           + [("proj", j, h) for j in range(2) for h in range(2)])
FRONT_B = [("v", u) for u in range(T // 2)] + [("proj", j, h) for j in range(2, 4) for h in range(2)]
BANKLESS = {"store_stats", "front_stats", "head_scale"}


def maxima(g):
    return [("score_max", g, n) for n in range(HG * T * 2)] + [("max_row", g)]


def bank_uses(slots):
    return {s: k for k, s in enumerate(s for slot in slots for s in slot if s[0] not in BANKLESS)}


def hybrid_kernel(nc, x, w0, q_gamma, q_beta, k_gamma, k_beta, w1, wagg, bagg, wgate, wexp, out):
    tokens = nc.dram_tensor("tokens_scratch", (B * N, C), F32).ap()
    logits_d = nc.dram_tensor("logits_scratch", (B, P, T * E), F32).ap()
    x_v = x.rearrange("b h w c -> b (h w) c").rearrange("b (t p) c -> b p t c", p=P)
    out_v = out.rearrange("b h w c -> b (h w) c").rearrange("b (t p) c -> b p t c", p=P)
    out_rows = out.rearrange("b h w c -> (b h w) c")
    tok_v = tokens.rearrange("(b t p) c -> b p t c", p=P, t=T)

    with ExitStack() as ctx:
        def sb(name, shape, dt=F32):
            return ctx.enter_context(nc.sbuf_tensor(name, shape, dt))

        ident = sb("ident", [P, P])
        ones = sb("ones", [P, P])
        gn_mean = sb("gn_mean", [P, P])
        head_mask = sb("head_mask", [P, CH, P])
        w0_sb = sb("w0_sb", [P, CH, 3 * C])
        w1T = sb("w1T", [P, CH, 3 * C])
        waggT = sb("waggT", [P, CH, C])
        bias = sb("bias", [P, C])
        gate_w = sb("gate_w", [P, CH, E])
        gb = sb("gb", [P, 4])

        setup_sems = ExitStack()
        with setup_sems:
            build_setup(nc, locals())

        phase = ExitStack()
        with phase:
            build_attention(nc, phase, locals())
        phase = ExitStack()
        with phase:
            build_experts(nc, phase, locals())


def build_setup(nc, env):
    ident, ones, gn_mean, head_mask = env["ident"], env["ones"], env["gn_mean"], env["head_mask"]
    w0_sb, w1T, waggT, bias, gate_w, gb = (env[k] for k in ("w0_sb", "w1T", "waggT", "bias", "gate_w", "gb"))
    with ExitStack() as ctx:
        def sem(name):
            return ctx.enter_context(nc.semaphore(name))

        w1_nat = ctx.enter_context(nc.sbuf_tensor("w1_nat", [P, 6, C], F32))
        wagg_nat = ctx.enter_context(nc.sbuf_tensor("wagg_nat", [P, CH, C], F32))
        bagg_row = ctx.enter_context(nc.sbuf_tensor("bagg_row", [1, C], F32))
        head_sum = ctx.enter_context(nc.sbuf_tensor("head_sum", [P, CH, 2 * H], F32))
        turned = [ctx.enter_context(nc.psum_tensor(f"turned{i}", [P, BANK], F32)) for i in range(5)]
        loaded, filled, constants = sem("loaded"), sem("filled"), sem("constants")
        turned_ready, dve_chain = sem("turned_ready"), sem("dve_chain")
        block = ctx.enter_context(nc.Block())

        @block.sync
        def _(sp):
            sp.dma_start(w0_sb[:, :, :], env["w0"].rearrange("(c p) n -> p c n", p=P)).then_inc(loaded, 16)
            sp.dma_start(w1_nat[:, :, :], env["w1"].rearrange("(c p) n -> p c n", p=P)).then_inc(loaded, 16)
            sp.dma_start(wagg_nat[:, :, :], env["wagg"].rearrange("(c p) n -> p c n", p=P)).then_inc(loaded, 16)
            sp.dma_start(gate_w[:, :, :], env["wgate"][0, :, :].rearrange("(c p) n -> p c n", p=P)).then_inc(loaded, 16)
            sp.dma_start(bagg_row[:, :], env["bagg"].rearrange("(a n) -> a n", a=1)).then_inc(loaded, 16)
            n = 5
            for col, v in enumerate(("q_gamma", "q_beta", "k_gamma", "k_beta")):
                for r in range(HG):
                    sp.dma_start(gb[DH * r:DH * (r + 1), col:col + 1],
                                 env[v].rearrange("(n a) -> n a", a=1)).then_inc(loaded, 16)
                    n += 1
            assert n == 5 + 4 * HG
            sp.wait_ge(loaded, 16 * n)

        @block.gpsimd
        def _(pool):
            pool.memset(ident[:, :], 0.0).then_inc(filled, 1)
            pool.memset(ones[:, :], 1.0).then_inc(filled, 1)
            pool.memset(gn_mean[:, :], 1.0 / GROUP).then_inc(filled, 1)
            pool.memset(head_mask[:, :, :], 1.0 / N).then_inc(filled, 1)
            pool.wait_ge(filled, 4)
            pool.affine_select(out=ident[:, :], in_=ident[:, :], compare_op=ALU.not_equal, fill=1.0,
                               base=0, pattern=[[-1, P]], channel_multiplier=1).then_inc(constants, 1)
            for n, (mat, width) in enumerate(((gn_mean[:, :], GROUP), (head_mask[:, :, :], DH))):
                blocks = P // width
                reps = [[0, CH]] if n else []
                view = mat.rearrange("p (g w) -> p g w", w=width) if not n else \
                    mat.rearrange("p c (g w) -> p c g w", w=width)
                pool.affine_select(out=view, in_=view, compare_op=ALU.is_ge, fill=0.0, base=0,
                                   pattern=[*reps, [-width, blocks], [0, width]],
                                   channel_multiplier=1).then_inc(constants, 1)
                pool.wait_ge(constants, 2 + 2 * n)
                pool.affine_select(out=view, in_=view, compare_op=ALU.is_ge, fill=0.0, base=width - 1,
                                   pattern=[*reps, [width, blocks], [0, width]],
                                   channel_multiplier=-1).then_inc(constants, 1)
            pool.wait_ge(constants, 5)

        @block.tensor
        def _(pe):
            pe.wait_ge(loaded, 16 * (5 + 4 * HG))
            pe.wait_ge(constants, 5)
            for c in range(CH):
                for o in range(6):
                    pe.transpose(turned[2 * c + o // 4][:, P * (o % 4):P * (o % 4 + 1)],
                                 w1_nat[:, o, P * c:P * (c + 1)], ident[:, :])
            for c in range(CH):
                for o in range(CH):
                    pe.transpose(turned[2 * c + 1][:, 2 * P + P * o:3 * P + P * o],
                                 wagg_nat[:, o, P * c:P * (c + 1)], ident[:, :])
            pe.matmul(turned[4][:, 0:C], ones[0:1, :], bagg_row[0:1, :], start=True, stop=True) \
              .then_inc(turned_ready, 1)

        @block.vector
        def _(dve):
            dve.wait_ge(loaded, 16 * (5 + 4 * HG))
            qk = w0_sb[:, :, 0:2 * C].rearrange("p c (h d) -> p c h d", d=DH)
            for c in range(CH):
                dve.tensor_reduce(head_sum[:, c, :], qk[:, c], AX.X, ALU.add).then_inc(dve_chain, 1)
            dve.wait_ge(dve_chain, 2)
            dve.tensor_scalar(head_sum[:, :, :], head_sum[:, :, :], 1.0 / DH, None, ALU.mult).then_inc(dve_chain, 1)
            dve.wait_ge(dve_chain, 3)
            for c in range(CH):
                dve.tensor_tensor(qk[:, c], qk[:, c], head_sum[:, c, :].unsqueeze(2).to_broadcast([P, 2 * H, DH]),
                                  ALU.subtract).then_inc(dve_chain, 1)
            dve.wait_ge(turned_ready, 1)
            for c in range(CH):
                dve.tensor_copy(w1T[:, c, 0:BANK], turned[2 * c][:, :]).then_inc(dve_chain, 1)
                dve.tensor_copy(w1T[:, c, BANK:3 * C], turned[2 * c + 1][:, 0:C]).then_inc(dve_chain, 1)
                dve.tensor_copy(waggT[:, c, :], turned[2 * c + 1][:, C:2 * C]).then_inc(dve_chain, 1)
            dve.tensor_copy(bias[:, :], turned[4][:, 0:C]).then_inc(dve_chain, 1)
            dve.wait_ge(dve_chain, 12)


class Chain:

    def __init__(self, dve, done):
        self.dve, self.done, self.count = dve, done, 0

    def __call__(self, instruction):
        instruction.then_inc(self.done, 1)
        self.count += 1
        self.dve.wait_ge(self.done, self.count)


def rsqrt(dve, link, v, y, half):
    link(dve.tensor_scalar(half.bitcast(I32), v.bitcast(I32), 1, None, ALU.logical_shift_right))
    link(dve.tensor_scalar(y.bitcast(I32), half.bitcast(I32), -1.0, float(RSQRT_SEED), ALU.mult, ALU.add))
    for _ in range(3):
        link(dve.scalar_tensor_tensor(out=half, in0=y, scalar=-0.5, in1=y, op0=ALU.mult, op1=ALU.mult))
        link(dve.tensor_tensor(half, half, v, ALU.mult))
        link(dve.scalar_tensor_tensor(out=y, in0=half, scalar=1.5, in1=y, op0=ALU.add, op1=ALU.mult))


def build_attention(nc, ctx, env):
    def sb(name, shape, dt=F32):
        return ctx.enter_context(nc.sbuf_tensor(name, shape, dt))

    key_stack = sb("key_stack", [P, H, N], F32R)
    query_stack = sb("query_stack", [P, H, N], F32R)
    hi = sb("hi", [P, 4, N])
    lo = sb("lo", [P, 4, N])
    v_sb = sb("v_sb", [P, T, C])
    v_next = sb("v_next", [P, T, C])
    x_sb = sb("x_sb", [P, T, C])
    chan = sb("chan", [P, CH, N])
    rows = sb("rows", [P, T, C])
    lin_out = sb("lin_out", [P, T, C])
    resid = sb("resid", [P, T, C])
    attn_T = sb("attn_T", [P, G, N])
    probs = sb("probs", [P, 2, HG * QB])
    squares = sb("squares", [P, 2, 2 * C])
    qT = hi[:, 0:2, :]
    qk0 = lo[:, :, :].rearrange("p j n -> p (j n)").rearrange("p (t n) -> p t n", n=2 * C)
    dots_sb = sb("dots_sb", [P, CH, P])
    sumv_sb = sb("sumv_sb", [P, C])
    x_sum = sb("x_sum", [P, CH, P])
    recip = sb("recip", [P, QB])
    bn6 = sb("bn6", [P, T, 6])
    mv = sb("mv", [P, T, 2])
    small = sb("small", [P, 8, CH])
    ss = sb("ss", [P, T, 2 * H])
    hr = sb("hr", [P, T, 2 * H])
    hh = sb("hh", [P, T, 2 * H])
    ln_v = sb("ln_v", [P, T])
    ln_r = sb("ln_r", [P, T])
    ln_h = sb("ln_h", [P, T])
    max2 = sb("max2", [P, HG * T, 2])
    max1 = sb("max1", [P, HG * T])
    max_rows = sb("max_rows", [HG * T, P], F32R)
    logits_sb = sb("logits_sb", [P, T * E])
    score_ps = [ctx.enter_context(nc.psum_tensor(f"scores{i}", [P, HG * QB], F32)) for i in range(2)]
    acc_ps = [ctx.enter_context(nc.psum_tensor(f"acc{i}", [P, BANK], F32)) for i in range(2)]
    shared_ps = [ctx.enter_context(nc.psum_tensor(f"shared{i}", [P, BANK], F32)) for i in range(2)]
    sems = {}

    def sem(name):
        if name not in sems:
            sems[name] = ctx.enter_context(nc.semaphore(name))
        return sems[name]

    names = ("x_loaded group_copied0 group_copied1 v_copied0 v_copied1 max_row_in0 max_row_in1 tokens_out "
             "logits_out full0 full1 read0 read1 scores_ready exp_done weighed acc_read mean_ready dev_ready "
             "xn_ready x_sum_ready squared squares_summed head_r_ready head_scaled dots_ready z_ready hi_ready "
             "z2_ready maxima_ready resid_ready dve_done stack_rows").split()
    sems = {n: ctx.enter_context(nc.semaphore(n)) for n in names}
    nums = sorted(s.num for s in sems.values())
    assert nums == list(range(nums[0], nums[-1] + 1))
    env = dict(env)
    env.update(locals())

    with nc.Block() as block:
        @block.vector
        def _(dve):
            dve.memset(key_stack[MAX_ROW:P, :, :].bitcast(F32), 0.0).then_inc(sems["stack_rows"], 1)
            dve.memset(query_stack[MAX_ROW:P, :, :].bitcast(F32), 0.0).then_inc(sems["stack_rows"], 1)
            dve.wait_ge(sems["stack_rows"], 2)
            dve.memset(key_stack[MAX_ROW:MAX_ROW + 1, :, :].bitcast(F32), 1.0).then_inc(sems["stack_rows"], 1)
            dve.wait_ge(sems["stack_rows"], 3)

    def ended():
        nc.all_engine_barrier()
        nc.gpsimd.sem_clear(range(nums[0], nums[-1] + 1))
        nc.all_engine_barrier()

    ended()
    build_batch(nc, env, 0, front=True)
    ended()
    build_batch(nc, env, 0, front=True, attend=True)
    ended()
    with nc.Fori(1, B - 1) as b:
        build_batch(nc, env, b, front=True, attend=True, store=True)
        ended()
    build_batch(nc, env, B - 1, attend=True, store=True)
    ended()
    build_batch(nc, env, B, store=True)
    ended()


def build_batch(nc, env, b, front=False, attend=False, store=False):
    s = env["sems"]
    nxt = b + 1 if attend else b
    first = (STORE if store else []) + (FRONT_A if front else [])
    second = FRONT_B if front else []
    if attend:
        half = UNITS // 2
        early, later = first[:T], maxima(1)
        slots = spread(merged(early, later[:T], 1.0) + merged(first[T:], later[T:]), half)
        slots += spread(merged(second, maxima(0)) if second else [], half)
    else:
        slots = [first + second + (maxima(0) if front else [])]
    assert not (attend and store) or all(("agg", t) in sum(slots[:T], []) for t in range(T))
    use = bank_uses(slots)
    (key_stack, query_stack, hi, lo, v_sb, v_next, x_sb, chan, rows, lin_out, resid, attn_T, probs, squares,
     qT, qk0, dots_sb, sumv_sb, x_sum, recip, bn6, mv, small, ss, hr, hh, ln_v, ln_r, ln_h, max2, max1,
     max_rows, logits_sb, score_ps, acc_ps, shared_ps) = (env[k] for k in (
        "key_stack query_stack hi lo v_sb v_next x_sb chan rows lin_out resid attn_T probs squares "
        "qT qk0 dots_sb sumv_sb x_sum recip bn6 mv small ss hr hh ln_v ln_r ln_h max2 max1 "
        "max_rows logits_sb score_ps acc_ps shared_ps").split())
    ident, ones, gn_mean, head_mask, w0_sb, w1T, waggT, bias, gate_w, gb = (env[k] for k in (
        "ident ones gn_mean head_mask w0_sb w1T waggT bias gate_w gb").split())
    STACK_DMAS = 6 * HG * 16
    LAST_X = ("xT", CH - 1, 1)

    def bank(step):
        k = use[step]
        return shared_ps[k % 2], k % 2, k // 2

    def await_full(eng, *step):
        ps, i, nth = bank(step)
        eng.wait_ge(s[f"full{i}"], nth + 1)
        return ps

    def read(instruction, *step):
        instruction.then_inc(s[f"read{bank(step)[1]}"], 1)

    def await_read(eng, *step):
        _, i, nth = bank(step)
        eng.wait_ge(s[f"read{i}"], nth + 1)

    with nc.Block() as block:

        @block.sync
        def _(sp):
            waits = []

            def copy_group(g):
                for r in range(HG):
                    h, src = HG * g + r, slice(DH * r, DH * (r + 1))
                    for quarter, q_part, k_part in ((0, hi, hi), (1, hi, lo), (2, lo, hi)):
                        dst = slice(DH * quarter, DH * (quarter + 1))
                        sp.dma_start(query_stack[dst, h, :].bitcast(F32), q_part[src, 2 * g, :]) \
                          .then_inc(s[f"group_copied{g}"], 16)
                        sp.dma_start(key_stack[dst, h, :].bitcast(F32), k_part[src, 2 * g + 1, :]) \
                          .then_inc(s[f"group_copied{g}"], 16)
                waits.append((f"group_copied{g}", STACK_DMAS))

            def copy_v(g):
                sp.dma_start(v_sb[:, :, P * g:P * (g + 1)], v_next[:, :, P * g:P * (g + 1)]) \
                  .then_inc(s[f"v_copied{g}"], 16)
                waits.append((f"v_copied{g}", 16))

            def shift_row(g):
                await_read(sp, "max_row", g)
                sp.dma_start(query_stack[MAX_ROW:MAX_ROW + 1, HG * g:HG * (g + 1), :].bitcast(F32),
                             max_rows[:, :].bitcast(F32)) \
                  .then_inc(s[f"max_row_in{g}"], 16)
                waits.append((f"max_row_in{g}", 16))

            if front:
                sp.dma_start(x_sb[:, :, :], env["x_v"][nxt, :, :, :]).then_inc(s["x_loaded"], 16)
                waits.append(("x_loaded", 16))
            if attend:
                copy_group(1)
                copy_v(1)
            if store:
                for h in range(2):
                    part = slice(T // 2 * h, T // 2 * (h + 1))
                    await_read(sp, "agg", part.stop - 2)
                    await_read(sp, "agg", part.stop - 1)
                    sp.dma_start(env["out_v"][b - 1, :, part, :], resid[:, part, :]).then_inc(s["tokens_out"], 16)
                    sp.dma_start(env["tok_v"][b - 1, :, part, :], resid[:, part, :]).then_inc(s["tokens_out"], 16)
                waits.append(("tokens_out", 64))
                await_read(sp, "gate")
                sp.dma_start(env["logits_d"][b - 1, :, :], logits_sb[:, :]).then_inc(s["logits_out"], 16)
                waits.append(("logits_out", 16))
            if attend:
                shift_row(1)
            if front:
                if attend:
                    sp.wait_ge(s["weighed"], UNITS // 2)
                for h in range(2):
                    await_read(sp, "proj", 1, h)
                copy_group(0)
                for u in range(2):
                    await_read(sp, "v", T // 2 - 2 + u)
                copy_v(0)
                shift_row(0)
            for name, value in waits:
                sp.wait_ge(s[name], value)

        @block.tensor
        def _(pe):
            def scores(u):
                g, qb, kt = u // (NQB * T), u // T % NQB, u % T
                if u == UNITS // 2:
                    pe.wait_ge(s["max_row_in1"], 16)
                if u >= 2:
                    pe.wait_ge(s["exp_done"], u - 1)
                for r in range(HG):
                    last = pe.matmul(score_ps[u % 2][:, QB * r:QB * (r + 1)],
                                     key_stack[:, HG * g + r, P * kt:P * (kt + 1)],
                                     query_stack[:, HG * g + r, QB * qb:QB * (qb + 1)], start=True, stop=True)
                last.then_inc(s["scores_ready"], 1)

            def weigh(u):
                g, blk, kt = u // (NQB * T), u // T, u % T
                if u == UNITS // 2:
                    pe.wait_ge(s["v_copied1"], 16)
                if kt == 0 and blk >= 2:
                    pe.wait_ge(s["acc_read"], blk - 1)
                pe.wait_ge(s["exp_done"], u + 1)
                acc, p = acc_ps[blk % 2], probs[:, u % 2, :]
                for r in range(HG):
                    pe.matmul(acc[DH * r:DH * (r + 1), 0:QB], v_sb[:, kt, P * g + DH * r:P * g + DH * (r + 1)],
                              p[:, QB * r:QB * (r + 1)], start=kt == 0, stop=kt == T - 1,
                              skip_group_check=True, tile_position=(0, DH * r))
                for r in range(HG):
                    last = pe.matmul(acc[DH * r:DH * (r + 1), QB:2 * QB], ones[:, 0:DH],
                                     p[:, QB * r:QB * (r + 1)], start=False, stop=kt == T - 1,
                                     skip_group_check=True, tile_position=(0, DH * r))
                last.then_inc(s["weighed"], 1)

            def transposes(ps, *blocks):
                for j, m in enumerate(blocks):
                    last = pe.transpose(ps[:, P * j:P * (j + 1)], m, ident[:, :])
                return last

            def product(out, pairs):
                for j, (stationary, moving) in enumerate(pairs):
                    last = pe.matmul(out, stationary, moving, start=j == 0, stop=j == len(pairs) - 1)
                return last

            def step(st):
                kind, *at = st
                if kind in BANKLESS:
                    return
                ps, i, nth = bank(st)
                if nth:
                    pe.wait_ge(s[f"read{i}"], nth)
                tok = [slice(P * t, P * (t + 1)) for t in range(T)]
                half = [slice(P * c, P * (c + 1)) for c in range(CH)]
                if kind == "score_max":
                    g, n = at
                    r, qt, kh = n // (2 * T), n // 2 % T, n % 2
                    if n == 0:
                        pe.wait_ge(s[f"group_copied{g}"], STACK_DMAS)
                    last = product(ps[:, :], [(query_stack[0:MAX_ROW, HG * g + r, tok[qt]],
                                               key_stack[0:MAX_ROW, HG * g + r, BANK * kh:BANK * (kh + 1)])])
                elif kind == "max_row":
                    pe.wait_ge(s["maxima_ready"], 2 if attend and at[0] == 0 else 1)
                    last = pe.transpose(ps[0:HG * T, 0:P], max1[:, :], ident[:, :])
                elif kind == "agg":
                    last = product(ps[:, 0:C], [(attn_T[:, c, tok[at[0]]], waggT[:, c, :]) for c in range(CH)])
                elif kind == "z2T":
                    pe.wait_ge(s["z2_ready"], 1)
                    last = transposes(ps, *(rows[:, at[0], half[c]] for c in range(CH)))
                elif kind == "gate":
                    for t in range(T - 2, T):
                        await_read(pe, "z2T", t)
                    for t in range(T):
                        last = product(ps[:, E * t:E * (t + 1)],
                                       [(chan[:, c, tok[t]], gate_w[:, c, :]) for c in range(CH)])
                elif kind == "xT":
                    c, h = at
                    pe.wait_ge(s["x_loaded"], 16)
                    last = transposes(ps, *(x_sb[:, 4 * h + j, half[c]] for j in range(4)))
                elif kind == "gmean":
                    pe.wait_ge(s["mean_ready"], 1)
                    last = product(ps[:, 0:CH], [(gn_mean[:, :], small[:, 0, :])])
                elif kind == "gvar":
                    pe.wait_ge(s["dev_ready"], 1)
                    last = product(ps[:, 0:CH], [(gn_mean[:, :], small[:, 3, :])])
                elif kind == "qk0":
                    pe.wait_ge(s["xn_ready"], 1)
                    last = product(ps[:, :], [(chan[:, c, tok[at[0]]], w0_sb[:, c, 0:2 * C]) for c in range(CH)])
                elif kind == "v0":
                    last = product(ps[:, 0:C],
                                   [(chan[:, c, tok[at[0]]], w0_sb[:, c, 2 * C:3 * C]) for c in range(CH)])
                elif kind == "sumv":
                    pe.wait_ge(s["x_sum_ready"], 1)
                    last = product(ps[:, 0:C], [(x_sum[:, c, :], w0_sb[:, c, 2 * C:3 * C]) for c in range(CH)])
                elif kind == "dots":
                    pe.wait_ge(s["head_scaled"], 2)
                    await_read(pe, "v0", T - 1)
                    for c in range(CH):
                        last = product(ps[:, half[c]], [(qk0[:, t, C + P * c:C + P * (c + 1)], rows[:, t, half[c]])
                                                        for t in range(T)])
                elif kind == "qT":
                    c, h = at
                    last = transposes(ps, *(qk0[:, 4 * h + j, half[c]] for j in range(4)))
                elif kind == "lin":
                    for h in range(2):
                        await_read(pe, "qT", CH - 1, h)
                    pe.wait_ge(s["dots_ready"], 1)
                    for c in range(CH):
                        last = product(ps[:, half[c]], [(qT[:, c, tok[at[0]]], dots_sb[:, c, :])])
                elif kind == "zT":
                    c, h = at
                    pe.wait_ge(s["z_ready"], 1)
                    last = transposes(ps, *(rows[:, 4 * h + j, half[c]] for j in range(4)))
                elif kind == "proj":
                    j, h = at
                    w = C * (j % 2) + P * (j // 2)
                    for hh_ in range(2):
                        await_read(pe, "zT", CH - 1, hh_)
                    last = product(ps[:, :], [(w1T[:, c, w:w + P], chan[:, c, BANK * h:BANK * (h + 1)])
                                              for c in range(CH)])
                elif kind == "v":
                    for j in range(2):
                        last = product(ps[:, C * j:C * (j + 1)],
                                       [(chan[:, c, tok[2 * at[0] + j]], w1T[:, c, 2 * C:3 * C]) for c in range(CH)])
                last.then_inc(s[f"full{i}"], 1)

            if attend:
                scores(0)
            for u, slot in enumerate(slots):
                if attend and u + 1 < UNITS and u + 1 != UNITS // 2:
                    scores(u + 1)
                for st in slot:
                    step(st)
                if attend:
                    if u + 1 == UNITS // 2:
                        scores(u + 1)
                    weigh(u)

        @block.scalar
        def _(act):
            def step(st):
                kind, *at = st
                if kind == "z2T":
                    ps = await_full(act, *st)
                    read(act.activation(chan[:, :, P * at[0]:P * (at[0] + 1)],
                                        ps[:, 0:C].rearrange("p (c n) -> p c n", c=CH), ACT.Copy), *st)
                elif kind in ("xT", "zT"):
                    c, h = at
                    ps = await_full(act, *st)
                    read(act.activation(chan[:, c, BANK * h:BANK * (h + 1)], ps[:, :], ACT.Copy), *st)
                elif kind == "qk0":
                    if at[0] == 0 and attend:
                        act.wait_ge(s["group_copied1"], STACK_DMAS)
                    ps = await_full(act, *st)
                    read(act.activation(qk0[:, at[0], :], ps[:, :], ACT.Copy), *st)
                elif kind == "v0":
                    ps = await_full(act, *st)
                    read(act.activation(rows[:, at[0], :], ps[:, 0:C], ACT.Copy), *st)
                elif kind == "qT":
                    c, h = at
                    ps = await_full(act, *st)
                    read(act.activation(qT[:, c, BANK * h:BANK * (h + 1)], ps[:, :], ACT.Identity,
                                        bias=gb[:, 1:2], scale=gb[:, 0:1]), *st)
                elif kind == "proj":
                    j, h = at
                    ps = await_full(act, *st)
                    act.activation(hi[:, j, BANK * h:BANK * (h + 1)].bitcast(F32R), ps[:, :], ACT.Copy) \
                       .then_inc(s["hi_ready"], 1)
                elif kind == "v":
                    ps = await_full(act, *st)
                    if at[0] == 0 and attend:
                        act.wait_ge(s["v_copied1"], 16)
                    read(act.activation(v_next[:, 2 * at[0]:2 * at[0] + 2, :],
                                        ps[:, :].rearrange("p (t n) -> p t n", t=2), ACT.Copy), *st)

            for u, slot in enumerate(slots):
                if attend:
                    act.wait_ge(s["scores_ready"], u + 1)
                    if u >= 2:
                        act.wait_ge(s["weighed"], u - 1)
                    act.activation(probs[:, u % 2, :], score_ps[u % 2][:, :], ACT.Exp, scale=DH ** -0.5) \
                       .then_inc(s["exp_done"], 1)
                for st in slot:
                    step(st)

        @block.gpsimd
        def _(pool):
            if attend:
                if store:
                    pool.wait_ge(s["tokens_out"], 64)
                    pool.wait_ge(s["z2_ready"], 1)
                for t in range(T):
                    pool.tensor_tensor(resid[:, t, :], lin_out[:, t, :], bias[:, :], ALU.add) \
                        .then_inc(s["resid_ready"], 1)
            if front:
                for t in range(T):
                    await_read(pool, "qk0", t)
                    if t >= 2:
                        pool.wait_ge(s["squares_summed"], t - 1)
                    pool.tensor_tensor(squares[:, t % 2, :], qk0[:, t, :], qk0[:, t, :], ALU.mult) \
                        .then_inc(s["squared"], 1)
                    if t % (T // 2) == T // 2 - 1:
                        pool.wait_ge(s["head_r_ready"], t // (T // 2) + 1)
                        for tt in range(t + 1 - T // 2, t + 1):
                            view = qk0[:, tt, :].rearrange("p (h d) -> p h d", d=DH)
                            last = pool.tensor_tensor(
                                view, view, hr[:, tt, :].unsqueeze(2).to_broadcast([P, 2 * H, DH]), ALU.mult)
                        last.then_inc(s["head_scaled"], 1)

        @block.vector
        def _(dve):
            link = Chain(dve, s["dve_done"])

            def layer_norm(src):
                link(dve.tensor_scalar(ln_v[:, :], mv[:, :, 1], LN_EPS, None, ALU.add))
                rsqrt(dve, link, ln_v[:, :], ln_r[:, :], ln_h[:, :])
                for t in range(T):
                    last = dve.tensor_scalar(rows[:, t, :], src[:, t, :], mv[:, t, 0:1], ln_r[:, t:t + 1],
                                             ALU.subtract, ALU.mult)
                return last

            def add_tokens(st, target, source):
                t = st[1]
                ps = await_full(dve, *st)
                read(dve.tensor_tensor(target[:, t, :], ps[:, 0:C], source[:, t, :], ALU.add), *st)
                await_read(dve, *st)
                link(dve.bn_stats(bn6[:, t, :], target[:, t, :]))
                link(dve.bn_aggr(mv[:, t, :], bn6[:, t, :]))

            def step(st):
                kind, *at = st
                if kind == "score_max":
                    g, n = at
                    r, qt, kh = n // (2 * T), n // 2 % T, n % 2
                    ps = await_full(dve, *st)
                    read(dve.tensor_reduce(max2[:, T * r + qt, kh:kh + 1], ps[:, :], AX.X, ALU.max), *st)
                elif kind == "max_row":
                    g = at[0]
                    for n in range(2):
                        await_read(dve, "score_max", g, 2 * HG * T - 2 + n)
                    dve.tensor_reduce(max1[:, :], max2[:, :, :], AX.X, ALU.max).then_inc(s["maxima_ready"], 1)
                    if attend and g == 0:
                        dve.wait_ge(s["max_row_in1"], 16)
                    ps = await_full(dve, *st)
                    read(dve.tensor_scalar(max_rows[:, :], ps[0:HG * T, 0:P], -1.0, None, ALU.mult), *st)
                elif kind == "agg":
                    add_tokens(st, resid, resid)
                elif kind == "store_stats":
                    layer_norm(resid).then_inc(s["z2_ready"], 1)
                elif kind == "gate":
                    ps = await_full(dve, *st)
                    read(dve.tensor_scalar(logits_sb[:, :], ps[:, 0:T * E], CLIP, None, ALU.max), *st)
                elif kind == "xT":
                    c, h = at
                    await_read(dve, *st)
                    link(dve.bn_stats(bn6[:, 2 * c + h, :], chan[:, c, BANK * h:BANK * (h + 1)]))
                    if h:
                        link(dve.bn_aggr(mv[:, c, :], bn6[:, 2 * c:2 * c + 2, :].rearrange("p a b -> p (a b)")))
                    if st == LAST_X:
                        dve.tensor_copy(small[:, 0, :], mv[:, 0:CH, 0]).then_inc(s["mean_ready"], 1)
                elif kind == "gmean":
                    ps = await_full(dve, *st)
                    read(dve.tensor_copy(small[:, 1, :], ps[:, 0:CH]), *st)
                    await_read(dve, *st)
                    link(dve.tensor_tensor(small[:, 2, :], small[:, 0, :], small[:, 1, :], ALU.subtract))
                    link(dve.tensor_tensor(small[:, 3, :], small[:, 2, :], small[:, 2, :], ALU.mult))
                    dve.tensor_tensor(small[:, 3, :], small[:, 3, :], mv[:, 0:CH, 1], ALU.add) \
                       .then_inc(s["dev_ready"], 1)
                elif kind == "gvar":
                    ps = await_full(dve, *st)
                    read(dve.tensor_scalar(small[:, 4, :], ps[:, 0:CH], LN_EPS, None, ALU.add), *st)
                    await_read(dve, *st)
                    rsqrt(dve, link, small[:, 4, :], small[:, 5, :], small[:, 6, :])
                    for c in range(CH):
                        last = dve.tensor_scalar(chan[:, c, :], chan[:, c, :], small[:, 1, c:c + 1],
                                                 small[:, 5, c:c + 1], ALU.subtract, ALU.mult)
                    last.then_inc(s["xn_ready"], 1)
                    link(dve.scalar_tensor_tensor(out=small[:, 7, :], in0=small[:, 2, :], scalar=float(N),
                                                  in1=small[:, 5, :], op0=ALU.mult, op1=ALU.mult))
                    for c in range(CH):
                        last = dve.tensor_scalar(x_sum[:, c, :], ones[:, :], small[:, 7, c:c + 1], None, ALU.mult)
                    last.then_inc(s["x_sum_ready"], 1)
                elif kind == "v0":
                    t = at[0]
                    dve.wait_ge(s["squared"], t + 1)
                    dve.tensor_reduce(ss[:, t, :], squares[:, t % 2, :].rearrange("p (h d) -> p h d", d=DH),
                                      AX.X, ALU.add).then_inc(s["squares_summed"], 1)
                elif kind == "head_scale":
                    part = slice(T // 2 * at[0], T // 2 * (at[0] + 1))
                    dve.wait_ge(s["squares_summed"], part.stop)
                    flat = [m[:, part, :].rearrange("p t h -> p (t h)") for m in (ss, hr, hh)]
                    link(dve.tensor_scalar(flat[0], flat[0], 1.0 / DH, LN_EPS, ALU.mult, ALU.add))
                    rsqrt(dve, link, *flat)
                    dve.wait_ge(s["squares_summed"], part.stop)
                    dve.sem_inc(s["head_r_ready"], 1)
                elif kind == "sumv":
                    ps = await_full(dve, *st)
                    read(dve.tensor_scalar(sumv_sb[:, :], ps[:, 0:C], gb[:, 3:4], None, ALU.mult), *st)
                elif kind == "dots":
                    await_read(dve, "sumv")
                    ps = await_full(dve, *st)
                    flat = dots_sb[:, :, :].rearrange("p c n -> p (c n)")
                    read(dve.scalar_tensor_tensor(out=flat, in0=ps[:, 0:C], scalar=gb[:, 2:3], in1=sumv_sb[:, :],
                                                  op0=ALU.mult, op1=ALU.add), *st)
                    await_read(dve, *st)
                    dve.tensor_tensor(flat, flat, head_mask[:, :, :].rearrange("p c n -> p (c n)"), ALU.mult) \
                       .then_inc(s["dots_ready"], 1)
                elif kind == "lin":
                    if at[0] == 0 and attend:
                        dve.wait_ge(s["resid_ready"], T)
                    add_tokens(st, lin_out, x_sb)
                elif kind == "front_stats":
                    layer_norm(lin_out).then_inc(s["z_ready"], 1)
                elif kind == "proj":
                    j, h = at
                    part = slice(BANK * h, BANK * (h + 1))
                    ps = await_full(dve, *st)
                    dve.wait_ge(s["hi_ready"], 2 * j + h + 1)
                    read(dve.tensor_tensor(lo[:, j, part].bitcast(F32R), ps[:, :], hi[:, j, part], ALU.subtract), *st)

            def normalise(blk):
                g, qb = blk // NQB, blk % NQB
                acc = acc_ps[blk % 2]
                dve.wait_ge(s["weighed"], T * (blk + 1))
                if blk:
                    dve.wait_ge(s["acc_read"], blk)
                link(dve.reciprocal(recip[:, :], acc[:, QB:2 * QB]))
                dve.tensor_tensor(attn_T[:, g, QB * qb:QB * (qb + 1)], acc[:, 0:QB], recip[:, :], ALU.mult) \
                   .then_inc(s["acc_read"], 1)

            if attend and store:
                pass
            for u, slot in enumerate(slots):
                if attend and u and u % T == 0:
                    normalise(u // T - 1)
                for st in slot:
                    step(st)
            if attend:
                normalise(G * NQB - 1)


def build_experts(nc, ctx, env):
    def sb(name, shape, dt=F32):
        return ctx.enter_context(nc.sbuf_tensor(name, shape, dt))

    def ps(name, shape):
        return ctx.enter_context(nc.psum_tensor(name, shape, F32))

    ident, ones = env["ident"], env["ones"]
    tokens, out_rows = env["tokens"], env["out_rows"]
    BE = B * E
    gates = sb("gates", [P, B, T, E])
    gates_t = sb("gates_t", [P, T, B, E])
    col = sb("col", [P, B, E])
    col_r = sb("col_r", [P, B, E])
    row = sb("row", [P, B * T])
    row_r = sb("row_r", [P, B * T])
    work = sb("work", [BE, 2, N])
    best = sb("best", [BE, M])
    best_i = sb("best_i", [BE, M], U32)
    best_f = sb("best_f", [BE, M])
    first_token = sb("first_token", [P, B], I32)
    first_token_f = sb("first_token_f", [P, B])
    slot_token = sb("slot_token", [P, E + 1, B], U32)
    slot_gate = sb("slot_gate", [P, E, B])
    now_token = sb("now_token", [P, B], U32)
    next_token = sb("next_token", [P, B], U32)
    now_gate = sb("now_gate", [P, B])
    w_sb = sb("w_sb", [P, E, CH, C])
    picked = sb("picked", [P, B, C])
    z = sb("z", [P, B, C])
    zT = sb("zT3", [P, B, CH, P])
    result = sb("result", [P, B, C])
    bn6 = sb("bn6e", [P, B, 6])
    mv = sb("mve", [P, B, 2])
    ln_v, ln_r, ln_h = sb("ln_ve", [P, B]), sb("ln_re", [P, B]), sb("ln_he", [P, B])
    sum_ps = ps("sum_ps", [P, BANK])
    wide_ps = ps("wide_ps", [P, 2 * BANK])
    zT_ps = [ps(f"zT_ps{i}", [P, BANK]) for i in range(2)]
    y_ps = [ps(f"y_ps{i}", [P, BANK]) for i in range(2)]
    names = ("logits_in w_in dve_done sums_ready gates_ready turned gates_copied lists_ready lists_turned "
             "iota_done chosen z_ready zT_ready zT_read y_ready result_ready now_ready").split()
    s = {n: ctx.enter_context(nc.semaphore(n + "_e")) for n in names}
    nums = sorted(x.num for x in s.values())
    assert nums == list(range(nums[0], nums[-1] + 1))
    s["picked_in"], s["scattered"] = (ctx.enter_context(nc.semaphore(n)) for n in ("picked_in", "scattered"))

    def ended():
        nc.all_engine_barrier()
        nc.gpsimd.sem_clear(range(nums[0], nums[-1] + 1))
        nc.all_engine_barrier()

    def gather(pool, index, b):
        pool.indirect_dma_start(picked[:, b, :], None, tokens[:, :],
                                bass.IndirectOffsetOnAxis(ap=index[:, b:b + 1], axis=0)).then_inc(s["picked_in"], 16)

    with nc.Block() as block:
        @block.sync
        def _(sp):
            sp.dma_start(gates[:, :, :, :].rearrange("p b t e -> p b (t e)"),
                         env["logits_d"].rearrange("b p n -> p b n")).then_inc(s["logits_in"], 16)
            sp.dma_start(w_sb[:, :, :, :], env["wexp"].rearrange("e (c p) o -> p e c o", p=P)).then_inc(s["w_in"], 16)
            sp.wait_ge(s["w_in"], 16)

        @block.tensor
        def _(pe):
            pe.wait_ge(s["logits_in"], 16)
            for it in range(SINKHORN_ITERS):
                if it:
                    pe.wait_ge(s["gates_ready"], it)
                pe.matmul(sum_ps[:, :], ones[:, :], gates[:, :, :, :].rearrange("p b t e -> p (b t e)"),
                          start=True, stop=True).then_inc(s["sums_ready"], 1)
            pe.wait_ge(s["gates_ready"], SINKHORN_ITERS)
            for t in range(T):
                last = pe.transpose(wide_ps[0:BE, P * t:P * (t + 1)],
                                    gates_t[:, t, :, :].rearrange("p b e -> p (b e)"), ident[:, :])
            last.then_inc(s["turned"], 1)
            pe.wait_ge(s["lists_ready"], 2)
            pe.transpose(zT_ps[0][:, 0:BE], best_f[:, :], ident[0:BE, 0:BE])
            pe.transpose(zT_ps[1][:, 0:BE], best[:, :], ident[0:BE, 0:BE]).then_inc(s["lists_turned"], 1)

        @block.gpsimd
        def _(pool):
            pool.iota(first_token[:, :], pattern=[[N, B]], base=0, channel_multiplier=0).then_inc(s["iota_done"], 1)
            pool.wait_ge(s["chosen"], 1)
            for b in range(B):
                gather(pool, next_token, b)
            pool.wait_ge(s["picked_in"], 16 * B)

        @block.vector
        def _(dve):
            link = Chain(dve, s["dve_done"])
            flat = gates[:, :, :, :].rearrange("p b t e -> p (b t e)")
            by_token = gates[:, :, :, :].rearrange("p b t e -> p (b t) e")
            dve.wait_ge(s["logits_in"], 16)
            for it in range(SINKHORN_ITERS):
                dve.wait_ge(s["sums_ready"], it + 1)
                link(dve.tensor_reduce(col[:, :, :], sum_ps[:, :].rearrange("p (b t e) -> p b e t", b=B, t=T),
                                       AX.X, ALU.add))
                link(dve.reciprocal(col_r[:, :, :], col[:, :, :]))
                link(dve.tensor_tensor(gates[:, :, :, :], gates[:, :, :, :],
                                       col_r[:, :, :].unsqueeze(2).to_broadcast([P, B, T, E]), ALU.mult))
                link(dve.tensor_reduce(row[:, :], by_token, AX.X, ALU.add))
                link(dve.reciprocal(row_r[:, :], row[:, :]))
                if it < SINKHORN_ITERS - 1:
                    dve.tensor_tensor(by_token, by_token, row_r[:, :].unsqueeze(2).to_broadcast([P, B * T, E]),
                                      ALU.mult).then_inc(s["gates_ready"], 1)
                else:
                    dve.tensor_tensor(gates_t[:, :, :, :].rearrange("p t b e -> p b t e"), gates[:, :, :, :],
                                      row_r[:, :].rearrange("p (b t) -> p b t", b=B).unsqueeze(3)
                                      .to_broadcast([P, B, T, E]), ALU.mult).then_inc(s["gates_ready"], 1)
                dve.wait_ge(s["gates_ready"], it + 1)
            dve.wait_ge(s["turned"], 1)
            link(dve.tensor_copy(work[:, 0, :], wide_ps[0:BE, :]))
            for r in range(M // 8):
                eight = slice(8 * r, 8 * (r + 1))
                src, dst = work[:, r % 2, :], work[:, (r + 1) % 2, :]
                link(dve.max(best[:, eight], src))
                link(dve.max_index(best_i[:, eight], best[:, eight], src))
                if r < M // 8 - 1:
                    link(dve.match_replace(dst, best[:, eight], src, -1.0))
            dve.sem_inc(s["lists_ready"], 1)
            dve.tensor_copy(best_f[:, :], best_i[:, :]).then_inc(s["lists_ready"], 1)
            dve.wait_ge(s["iota_done"], 1)
            link(dve.tensor_copy(first_token_f[:, :], first_token[:, :]))
            dve.wait_ge(s["lists_turned"], 1)
            link(dve.tensor_tensor(slot_token[:, 0:E, :].rearrange("p e b -> p b e"),
                                   zT_ps[0][:, 0:BE].rearrange("p (b e) -> p b e", b=B),
                                   first_token_f[:, :].unsqueeze(2).to_broadcast([P, B, E]), ALU.add))
            link(dve.tensor_copy(slot_gate[:, :, :].rearrange("p e b -> p b e"),
                                 zT_ps[1][:, 0:BE].rearrange("p (b e) -> p b e", b=B)))
            link(dve.tensor_copy(slot_token[:, E, :], slot_token[:, 0, :]))
            dve.tensor_copy(next_token[:, :], slot_token[:, 0, :]).then_inc(s["chosen"], 1)
            dve.wait_ge(s["chosen"], 1)

    ended()
    with nc.Fori(0, E) as e:
        with nc.Block() as block:
            @block.vector
            def _(dve):
                link = Chain(dve, s["dve_done"])
                dve.tensor_copy(now_token[:, :], slot_token[:, bass.ds(e, 1), :].rearrange("p e b -> p (e b)"))
                dve.tensor_copy(now_gate[:, :], slot_gate[:, bass.ds(e, 1), :].rearrange("p e b -> p (e b)"))
                dve.tensor_copy(next_token[:, :], slot_token[:, bass.ds(e + 1, 1), :].rearrange("p e b -> p (e b)")) \
                   .then_inc(s["now_ready"], 1)
                for b in range(B):
                    link(dve.bn_stats(bn6[:, b, :], picked[:, b, :]))
                    link(dve.bn_aggr(mv[:, b, :], bn6[:, b, :]))
                link(dve.tensor_scalar(ln_v[:, :], mv[:, :, 1], LN_EPS, None, ALU.add))
                rsqrt(dve, link, ln_v[:, :], ln_r[:, :], ln_h[:, :])
                for b in range(B):
                    dve.tensor_scalar(z[:, b, :], picked[:, b, :], mv[:, b, 0:1], ln_r[:, b:b + 1],
                                      ALU.subtract, ALU.mult).then_inc(s["z_ready"], 1)
                for b in range(B):
                    dve.wait_ge(s["y_ready"], b + 1)
                    dve.scalar_tensor_tensor(out=result[:, b, :], in0=y_ps[b % 2][:, 0:C], scalar=now_gate[:, b:b + 1],
                                             in1=picked[:, b, :], op0=ALU.mult, op1=ALU.add) \
                       .then_inc(s["result_ready"], 1)

            @block.tensor
            def _(pe):
                def turn(b):
                    pe.wait_ge(s["z_ready"], b + 1)
                    if b >= 2:
                        pe.wait_ge(s["zT_read"], b - 1)
                    for c in range(CH):
                        last = pe.transpose(zT_ps[b % 2][:, P * c:P * (c + 1)], z[:, b, P * c:P * (c + 1)], ident[:, :])
                    last.then_inc(s["zT_ready"], 1)

                def multiply(b):
                    pe.wait_ge(s["zT_read"], b + 1)
                    if b >= 2:
                        pe.wait_ge(s["result_ready"], b - 1)
                    for c in range(CH):
                        last = pe.matmul(y_ps[b % 2][:, 0:C], zT[:, b, c, :],
                                         w_sb[:, bass.ds(e, 1), c, :].rearrange("p e o -> p (e o)"),
                                         start=c == 0, stop=c == CH - 1)
                    last.then_inc(s["y_ready"], 1)

                turn(0)
                for b in range(B):
                    if b + 1 < B:
                        turn(b + 1)
                    multiply(b)

            @block.scalar
            def _(act):
                for b in range(B):
                    act.wait_ge(s["zT_ready"], b + 1)
                    act.activation(zT[:, b, :, :].rearrange("p c n -> p (c n)"), zT_ps[b % 2][:, 0:C], ACT.Copy) \
                       .then_inc(s["zT_read"], 1)

            @block.gpsimd
            def _(pool):
                pool.wait_ge(s["now_ready"], 1)
                for b in range(B):
                    pool.wait_ge(s["result_ready"], b + 1)
                    pool.indirect_dma_start(out_rows[:, :], bass.IndirectOffsetOnAxis(ap=now_token[:, b:b + 1], axis=0),
                                            result[:, b, :], None).then_inc(s["scattered"], 16)
                    gather(pool, next_token, b)
                pool.wait_ge(s["scattered"], (e + 1) * (16 * B))
                pool.wait_ge(s["picked_in"], (e + 2) * (16 * B))
        ended()


_INS = ['x', 'L0_conv_w_qkv', 'L0_conv_q_gamma', 'L0_conv_q_beta', 'L0_conv_k_gamma', 'L0_conv_k_beta',
        'L1_attn_w_qkv', 'L1_attn_w_agg', 'L1_attn_b_agg', 'L1_ffn_gate_weight', 'L1_ffn_experts']
_OUTS = [((8, 32, 32, 256), 'float32')]


def kernel(**inputs):
    import numpy as _np
    import concourse.bacc as _bacc
    from concourse import mybir as _mybir
    from concourse.bass_utils import run_bass_kernel_spmd as _run

    nc = _bacc.Bacc("TRN2", target_bir_lowering=False, num_devices=1)
    arrays, args = {}, []
    for name in _INS:
        a = _np.ascontiguousarray(inputs[name])
        arrays[f"in_{name}_dram"] = a
        args.append(nc.dram_tensor(f"in_{name}_dram", a.shape, _mybir.dt.from_np(a.dtype), kind="ExternalInput").ap())
    for i, (shape, dtype) in enumerate(_OUTS):
        dt = _mybir.dt.from_np(_np.dtype(dtype))
        args.append(nc.dram_tensor(f"out_{i}_dram", shape, dt, kind="ExternalOutput").ap())
    hybrid_kernel(nc, *args)
    r = _run(nc, [arrays], core_ids=[0])
    return r.results[0]["out_0_dram"]
```

```python
import numpy as np
import concourse.bass as bass
from concourse import mybir
from contextlib import ExitStack

F32 = mybir.dt.float32
F32R = mybir.dt.float32r
I32 = mybir.dt.int32
U32 = mybir.dt.uint32
ALU = mybir.AluOpType
ACT = mybir.ActivationFunctionType
AX = mybir.AxisListType

P = 128
B = 8
N = 1024
C = 256
T = N // P
CH = C // P
H = 8
DH = C // H
HG = P // DH
G = H // HG
E = 8
M = N // E
GROUP = C // 32
BANK = 512
QB = 256
NQB = N // QB
BLOCK_UNITS = T
UNITS = G * NQB * BLOCK_UNITS
SINKHORN_ITERS = 8
LN_EPS = 1e-5
CLIP = 1e-6
MAX_ROW = 3 * DH
RSQRT_SEED = 0x5F3759DF
SAFE_SCORE = 64.0


def spread(steps, slots):
    return [steps[len(steps) * u // slots:len(steps) * (u + 1) // slots] for u in range(slots)]


STORE = [("agg", t) for t in range(T)] + [("store_stats",)] + [("z2T", t) for t in range(T)] + [("gate",)]
FRONT = ([("xT", c, h) for c in range(CH) for h in range(2)] + [("gmean",), ("gvar",)]
         + [(k, t) for t in range(T // 2) for k in ("qk0", "v0")] + [("head_scale", 0)]
         + [(k, t) for t in range(T // 2, T) for k in ("qk0", "v0")] + [("head_scale", 1)]
         + [("sumv",), ("dots",)] + [("qT", c, h) for c in range(CH) for h in range(2)]
         + [("lin", t) for t in range(T)] + [("front_stats",)]
         + [("zT", c, h) for c in range(CH) for h in range(2)]
         + [("proj", j, h) for j in range(4) for h in range(2)]
         + [x for u in range(T // 2) for x in (("v", u), ("norms", 2 * u), ("norms", 2 * u + 1))] + [("bound",)])
BANKLESS = {"store_stats", "front_stats", "head_scale"}


def bank_uses(slots):
    return {s: k for k, s in enumerate(s for slot in slots for s in slot if s[0] not in BANKLESS)}


def hybrid_kernel(nc, x, w0, q_gamma, q_beta, k_gamma, k_beta, w1, wagg, bagg, wgate, wexp, out):
    tokens = nc.dram_tensor("tokens_scratch", (B * N, C), F32).ap()
    logits_d = nc.dram_tensor("logits_scratch", (B, P, T * E), F32).ap()
    x_v = x.rearrange("b h w c -> b (h w) c").rearrange("b (t p) c -> b p t c", p=P)
    out_v = out.rearrange("b h w c -> b (h w) c").rearrange("b (t p) c -> b p t c", p=P)
    out_rows = out.rearrange("b h w c -> (b h w) c")
    tok_v = tokens.rearrange("(b t p) c -> b p t c", p=P, t=T)

    with ExitStack() as ctx:
        def sb(name, shape, dt=F32):
            return ctx.enter_context(nc.sbuf_tensor(name, shape, dt))

        ident = sb("ident", [P, P])
        ones = sb("ones", [P, P])
        gn_mean = sb("gn_mean", [P, P])
        head_mask = sb("head_mask", [P, CH, P])
        w0_sb = sb("w0_sb", [P, CH, 3 * C])
        w1T = sb("w1T", [P, CH, 3 * C])
        waggT = sb("waggT", [P, CH, C])
        bias = sb("bias", [P, C])
        gate_w = sb("gate_w", [P, CH, E])
        gb = sb("gb", [P, 4])

        setup_sems = ExitStack()
        with setup_sems:
            build_setup(nc, locals())

        phase = ExitStack()
        with phase:
            build_attention(nc, phase, locals())
        phase = ExitStack()
        with phase:
            build_experts(nc, phase, locals())


def build_setup(nc, env):
    ident, ones, gn_mean, head_mask = env["ident"], env["ones"], env["gn_mean"], env["head_mask"]
    w0_sb, w1T, waggT, bias, gate_w, gb = (env[k] for k in ("w0_sb", "w1T", "waggT", "bias", "gate_w", "gb"))
    with ExitStack() as ctx:
        def sem(name):
            return ctx.enter_context(nc.semaphore(name))

        w1_nat = ctx.enter_context(nc.sbuf_tensor("w1_nat", [P, 6, C], F32))
        wagg_nat = ctx.enter_context(nc.sbuf_tensor("wagg_nat", [P, CH, C], F32))
        bagg_row = ctx.enter_context(nc.sbuf_tensor("bagg_row", [1, C], F32))
        head_sum = ctx.enter_context(nc.sbuf_tensor("head_sum", [P, CH, 2 * H], F32))
        turned = [ctx.enter_context(nc.psum_tensor(f"turned{i}", [P, BANK], F32)) for i in range(5)]
        loaded, filled, constants = sem("loaded"), sem("filled"), sem("constants")
        turned_ready, dve_chain = sem("turned_ready"), sem("dve_chain")
        block = ctx.enter_context(nc.Block())

        @block.sync
        def _(sp):
            sp.dma_start(w0_sb[:, :, :], env["w0"].rearrange("(c p) n -> p c n", p=P)).then_inc(loaded, 16)
            sp.dma_start(w1_nat[:, :, :], env["w1"].rearrange("(c p) n -> p c n", p=P)).then_inc(loaded, 16)
            sp.dma_start(wagg_nat[:, :, :], env["wagg"].rearrange("(c p) n -> p c n", p=P)).then_inc(loaded, 16)
            sp.dma_start(gate_w[:, :, :], env["wgate"][0, :, :].rearrange("(c p) n -> p c n", p=P)).then_inc(loaded, 16)
            sp.dma_start(bagg_row[:, :], env["bagg"].rearrange("(a n) -> a n", a=1)).then_inc(loaded, 16)
            n = 5
            for col, v in enumerate(("q_gamma", "q_beta", "k_gamma", "k_beta")):
                for r in range(HG):
                    sp.dma_start(gb[DH * r:DH * (r + 1), col:col + 1],
                                 env[v].rearrange("(n a) -> n a", a=1)).then_inc(loaded, 16)
                    n += 1
            assert n == 5 + 4 * HG
            sp.wait_ge(loaded, 16 * n)

        @block.gpsimd
        def _(pool):
            pool.memset(ident[:, :], 0.0).then_inc(filled, 1)
            pool.memset(ones[:, :], 1.0).then_inc(filled, 1)
            pool.memset(gn_mean[:, :], 1.0 / GROUP).then_inc(filled, 1)
            pool.memset(head_mask[:, :, :], 1.0 / N).then_inc(filled, 1)
            pool.wait_ge(filled, 4)
            pool.affine_select(out=ident[:, :], in_=ident[:, :], compare_op=ALU.not_equal, fill=1.0,
                               base=0, pattern=[[-1, P]], channel_multiplier=1).then_inc(constants, 1)
            for n, (mat, width) in enumerate(((gn_mean[:, :], GROUP), (head_mask[:, :, :], DH))):
                blocks = P // width
                reps = [[0, CH]] if n else []
                view = mat.rearrange("p (g w) -> p g w", w=width) if not n else \
                    mat.rearrange("p c (g w) -> p c g w", w=width)
                pool.affine_select(out=view, in_=view, compare_op=ALU.is_ge, fill=0.0, base=0,
                                   pattern=[*reps, [-width, blocks], [0, width]],
                                   channel_multiplier=1).then_inc(constants, 1)
                pool.wait_ge(constants, 2 + 2 * n)
                pool.affine_select(out=view, in_=view, compare_op=ALU.is_ge, fill=0.0, base=width - 1,
                                   pattern=[*reps, [width, blocks], [0, width]],
                                   channel_multiplier=-1).then_inc(constants, 1)
            pool.wait_ge(constants, 5)

        @block.tensor
        def _(pe):
            pe.wait_ge(loaded, 16 * (5 + 4 * HG))
            pe.wait_ge(constants, 5)
            for c in range(CH):
                for o in range(6):
                    pe.transpose(turned[2 * c + o // 4][:, P * (o % 4):P * (o % 4 + 1)],
                                 w1_nat[:, o, P * c:P * (c + 1)], ident[:, :])
            for c in range(CH):
                for o in range(CH):
                    pe.transpose(turned[2 * c + 1][:, 2 * P + P * o:3 * P + P * o],
                                 wagg_nat[:, o, P * c:P * (c + 1)], ident[:, :])
            pe.matmul(turned[4][:, 0:C], ones[0:1, :], bagg_row[0:1, :], start=True, stop=True) \
              .then_inc(turned_ready, 1)

        @block.vector
        def _(dve):
            dve.wait_ge(loaded, 16 * (5 + 4 * HG))
            qk = w0_sb[:, :, 0:2 * C].rearrange("p c (h d) -> p c h d", d=DH)
            for c in range(CH):
                dve.tensor_reduce(head_sum[:, c, :], qk[:, c], AX.X, ALU.add).then_inc(dve_chain, 1)
            dve.wait_ge(dve_chain, 2)
            dve.tensor_scalar(head_sum[:, :, :], head_sum[:, :, :], 1.0 / DH, None, ALU.mult).then_inc(dve_chain, 1)
            dve.wait_ge(dve_chain, 3)
            for c in range(CH):
                dve.tensor_tensor(qk[:, c], qk[:, c], head_sum[:, c, :].unsqueeze(2).to_broadcast([P, 2 * H, DH]),
                                  ALU.subtract).then_inc(dve_chain, 1)
            dve.wait_ge(turned_ready, 1)
            for c in range(CH):
                dve.tensor_copy(w1T[:, c, 0:BANK], turned[2 * c][:, :]).then_inc(dve_chain, 1)
                dve.tensor_copy(w1T[:, c, BANK:3 * C], turned[2 * c + 1][:, 0:C]).then_inc(dve_chain, 1)
                dve.tensor_copy(waggT[:, c, :], turned[2 * c + 1][:, C:2 * C]).then_inc(dve_chain, 1)
            dve.tensor_copy(bias[:, :], turned[4][:, 0:C]).then_inc(dve_chain, 1)
            dve.wait_ge(dve_chain, 12)


class Chain:

    def __init__(self, dve, done):
        self.dve, self.done, self.count = dve, done, 0

    def __call__(self, instruction):
        instruction.then_inc(self.done, 1)
        self.count += 1
        self.dve.wait_ge(self.done, self.count)


def rsqrt(dve, link, v, y, half):
    link(dve.tensor_scalar(half.bitcast(I32), v.bitcast(I32), 1, None, ALU.logical_shift_right))
    link(dve.tensor_scalar(y.bitcast(I32), half.bitcast(I32), -1.0, float(RSQRT_SEED), ALU.mult, ALU.add))
    for _ in range(3):
        link(dve.scalar_tensor_tensor(out=half, in0=y, scalar=-0.5, in1=y, op0=ALU.mult, op1=ALU.mult))
        link(dve.tensor_tensor(half, half, v, ALU.mult))
        link(dve.scalar_tensor_tensor(out=y, in0=half, scalar=1.5, in1=y, op0=ALU.add, op1=ALU.mult))


def build_attention(nc, ctx, env):
    def sb(name, shape, dt=F32):
        return ctx.enter_context(nc.sbuf_tensor(name, shape, dt))

    key_stack = sb("key_stack", [P, H, N], F32R)
    query_stack = sb("query_stack", [P, H, N], F32R)
    hi = sb("hi", [P, 4, N])
    lo = sb("lo", [P, 4, N])
    v_sb = sb("v_sb", [P, T, C])
    v_next = sb("v_next", [P, T, C])
    x_sb = sb("x_sb", [P, T, C])
    chan = sb("chan", [P, CH, N])
    rows = sb("rows", [P, T, C])
    lin_out = sb("lin_out", [P, T, C])
    resid = sb("resid", [P, T, C])
    attn_T = sb("attn_T", [P, G, N])
    probs = sb("probs", [P, 3, HG * QB])
    prob_sum = sb("prob_sum", [P, 2, HG * QB])
    acc_sb = sb("acc_sb", [P, BANK])
    head_ones = sb("head_ones", [P, P], F32R)
    norm_sq = sb("norm_sq", [P, BANK], F32R)
    norm_max = sb("norm_max", [P, 4, 2])
    bound = sb("bound", [P, 8])
    shifted = sb("shifted", [1, 1], I32)
    squares = v_next[:, 0:4, :].rearrange("p (i a) n -> p i (a n)", i=2)
    qT = hi[:, 0:2, :]
    qk0 = lo[:, :, :].rearrange("p j n -> p (j n)").rearrange("p (t n) -> p t n", n=2 * C)
    dots_sb = sb("dots_sb", [P, CH, P])
    sumv_sb = sb("sumv_sb", [P, C])
    x_sum = sb("x_sum", [P, CH, P])
    bn6 = sb("bn6", [P, T, 6])
    mv = sb("mv", [P, T, 2])
    small = sb("small", [P, 8, CH])
    ss = sb("ss", [P, T, 2 * H])
    hr = sb("hr", [P, T, 2 * H])
    hh = sb("hh", [P, T, 2 * H])
    ln_v = sb("ln_v", [P, T])
    ln_r = sb("ln_r", [P, T])
    ln_h = sb("ln_h", [P, T])
    max2 = probs[:, 0, 0:2 * HG * T].rearrange("p (n a) -> p n a", a=2)
    max1 = probs[:, 1, 0:HG * T]
    max_rows = probs[0:HG * T, 2, 0:P]
    logits_sb = sb("logits_sb", [P, T * E])
    score_ps = [ctx.enter_context(nc.psum_tensor(f"scores{i}", [P, HG * QB], F32)) for i in range(2)]
    acc_ps = [ctx.enter_context(nc.psum_tensor(f"acc{i}", [P, BANK], F32)) for i in range(2)]
    shared_ps = [ctx.enter_context(nc.psum_tensor(f"shared{i}", [P, BANK], F32)) for i in range(2)]
    sems = {}

    def sem(name):
        if name not in sems:
            sems[name] = ctx.enter_context(nc.semaphore(name))
        return sems[name]

    names = ("x_loaded group_copied0 group_copied1 v_copied0 v_copied1 max_row_in0 max_row_in1 tokens_out "
             "logits_out full0 full1 read0 read1 scores_ready exp_done weighed mean_ready dev_ready "
             "xn_ready x_sum_ready squared squares_summed head_r_ready head_scaled dots_ready z_ready hi_ready "
             "z2_ready maxima_ready resid_ready dve_done stack_rows summed blocks_done acc_copied norm_squared "
             "bound_ready shift_known attn_ready recip_ready").split()
    sems = {n: ctx.enter_context(nc.semaphore(n)) for n in names}
    nums = sorted(s.num for s in sems.values())
    assert nums == list(range(nums[0], nums[-1] + 1))
    env = dict(env)
    env.update(locals())

    with nc.Block() as block:
        @block.vector
        def _(dve):
            dve.memset(key_stack[MAX_ROW:P, :, :].bitcast(F32), 0.0).then_inc(sems["stack_rows"], 1)
            dve.memset(query_stack[MAX_ROW:P, :, :].bitcast(F32), 0.0).then_inc(sems["stack_rows"], 1)
            dve.wait_ge(sems["stack_rows"], 2)
            dve.memset(key_stack[MAX_ROW:MAX_ROW + 1, :, :].bitcast(F32), 1.0).then_inc(sems["stack_rows"], 1)
            dve.tensor_scalar(head_ones[:, :], env["head_mask"][:, 0, :], float(N), None, ALU.mult) \
               .then_inc(sems["stack_rows"], 1)
            dve.wait_ge(sems["stack_rows"], 4)

    def ended():
        nc.all_engine_barrier()
        nc.gpsimd.sem_clear(range(nums[0], nums[-1] + 1))
        nc.all_engine_barrier()

    def attended(b, **work):
        needs_shift = nc.values_load(shifted[0:1, 0:1], min_val=0, max_val=1)
        with nc.If(needs_shift > 0):
            build_shift(nc, env)
            ended()
        build_batch(nc, env, b, attend=True, **work)
        ended()
        with nc.If(needs_shift > 0):
            with nc.Block() as block:
                @block.vector
                def _(dve):
                    dve.memset(query_stack[MAX_ROW:MAX_ROW + 1, :, :].bitcast(F32), 0.0) \
                       .then_inc(sems["stack_rows"], 1)
                    dve.wait_ge(sems["stack_rows"], 1)

                for engine in (block.sync, block.tensor, block.scalar, block.gpsimd):
                    @engine
                    def _(eng):
                        eng.wait_ge(sems["stack_rows"], 1)
            ended()

    ended()
    build_batch(nc, env, 0, front=True)
    ended()
    attended(0, front=True)
    with nc.Fori(1, B - 1) as b:
        attended(b, front=True, store=True)
    attended(B - 1, store=True)
    build_batch(nc, env, B, store=True)
    ended()


def copy_group(sp, env, g):
    hi, lo, query_stack, key_stack, s = (env[k] for k in ("hi", "lo", "query_stack", "key_stack", "sems"))
    for r in range(HG):
        h, src = HG * g + r, slice(DH * r, DH * (r + 1))
        for quarter, q_part, k_part in ((0, hi, hi), (1, hi, lo), (2, lo, hi)):
            dst = slice(DH * quarter, DH * (quarter + 1))
            sp.dma_start(query_stack[dst, h, :].bitcast(F32), q_part[src, 2 * g, :]) \
              .then_inc(s[f"group_copied{g}"], 16)
            sp.dma_start(key_stack[dst, h, :].bitcast(F32), k_part[src, 2 * g + 1, :]) \
              .then_inc(s[f"group_copied{g}"], 16)


STACK_DMAS = 6 * HG * 16


def build_shift(nc, env):
    s, ident = env["sems"], env["ident"]
    query_stack, key_stack, max2, max1, max_rows, shared_ps = (
        env[k] for k in ("query_stack", "key_stack", "max2", "max1", "max_rows", "shared_ps"))
    TILES = HG * T * 2
    USES = TILES + 1

    def full(eng, k):
        eng.wait_ge(s[f"full{k % 2}"], k // 2 + 1)
        return shared_ps[k % 2]

    with nc.Block() as block:
        @block.sync
        def _(sp):
            copy_group(sp, env, 1)
            for g in range(G):
                k = g * USES + TILES
                sp.wait_ge(s[f"read{k % 2}"], k // 2 + 1)
                sp.dma_start(query_stack[MAX_ROW:MAX_ROW + 1, HG * g:HG * (g + 1), :].bitcast(F32),
                             max_rows[:, :]).then_inc(s[f"max_row_in{g}"], 16)
                sp.wait_ge(s[f"max_row_in{g}"], 16)

        @block.tensor
        def _(pe):
            pe.wait_ge(s["group_copied1"], STACK_DMAS)
            for g in range(G):
                for n in range(USES):
                    k = g * USES + n
                    r, qt, kh = n // (2 * T), n // 2 % T, n % 2
                    if k >= 2:
                        pe.wait_ge(s[f"read{k % 2}"], k // 2)
                    if n < TILES:
                        last = pe.matmul(shared_ps[k % 2][:, :],
                                         query_stack[0:MAX_ROW, HG * g + r, P * qt:P * (qt + 1)],
                                         key_stack[0:MAX_ROW, HG * g + r, BANK * kh:BANK * (kh + 1)],
                                         start=True, stop=True)
                    else:
                        pe.wait_ge(s["maxima_ready"], g + 1)
                        last = pe.transpose(shared_ps[k % 2][0:HG * T, 0:P], max1[:, :], ident[:, :])
                    last.then_inc(s[f"full{k % 2}"], 1)

        @block.vector
        def _(dve):
            for g in range(G):
                for n in range(USES):
                    k = g * USES + n
                    if n < TILES:
                        ps = full(dve, k)
                        dve.tensor_reduce(max2[:, n // 2, n % 2:n % 2 + 1], ps[:, :], AX.X, ALU.max) \
                           .then_inc(s[f"read{k % 2}"], 1)
                        continue
                    for j in (k - 2, k - 1):
                        dve.wait_ge(s[f"read{j % 2}"], j // 2 + 1)
                    dve.tensor_reduce(max1[:, :], max2[:, :, :], AX.X, ALU.max).then_inc(s["maxima_ready"], 1)
        @block.scalar
        def _(act):
            for g in range(G):
                k = g * USES + TILES
                if g:
                    act.wait_ge(s["max_row_in0"], 16)
                ps = full(act, k)
                act.activation(max_rows.bitcast(F32R), ps[0:HG * T, 0:P], ACT.Copy, scale=-1.0) \
                   .then_inc(s[f"read{k % 2}"], 1)

        @block.gpsimd
        def _(pool):
            for g in range(G):
                pool.wait_ge(s[f"max_row_in{g}"], 16)


def build_batch(nc, env, b, front=False, attend=False, store=False):
    s = env["sems"]
    nxt = b + 1 if attend else b
    steps = (STORE if store else []) + (FRONT if front else [])
    dealt = (UNITS if front else 2 * T) if attend else 1
    slots = spread(steps, dealt) + [[]] * (UNITS - dealt if attend else 0)
    assert not (attend and store) or all(("agg", t) in sum(slots[:T], []) for t in range(T))
    use = bank_uses(slots)
    (key_stack, query_stack, hi, lo, v_sb, v_next, x_sb, chan, rows, lin_out, resid, attn_T, probs, squares,
     qT, qk0, dots_sb, sumv_sb, x_sum, bn6, mv, small, ss, hr, hh, ln_v, ln_r, ln_h,
     prob_sum, acc_sb, head_ones, norm_sq, norm_max, bound, shifted, logits_sb, score_ps, acc_ps, shared_ps) = (env[k] for k in (
        "key_stack query_stack hi lo v_sb v_next x_sb chan rows lin_out resid attn_T probs squares "
        "qT qk0 dots_sb sumv_sb x_sum bn6 mv small ss hr hh ln_v ln_r ln_h "
        "prob_sum acc_sb head_ones norm_sq norm_max bound shifted logits_sb score_ps acc_ps shared_ps").split())
    ident, ones, gn_mean, head_mask, w0_sb, w1T, waggT, bias, gate_w, gb = (env[k] for k in (
        "ident ones gn_mean head_mask w0_sb w1T waggT bias gate_w gb").split())
    LAST_X = ("xT", CH - 1, 1)

    def bank(step):
        k = use[step]
        return shared_ps[k % 2], k % 2, k // 2

    def await_full(eng, *step):
        ps, i, nth = bank(step)
        eng.wait_ge(s[f"full{i}"], nth + 1)
        return ps

    def read(instruction, *step):
        instruction.then_inc(s[f"read{bank(step)[1]}"], 1)

    def await_read(eng, *step):
        _, i, nth = bank(step)
        eng.wait_ge(s[f"read{i}"], nth + 1)

    with nc.Block() as block:

        @block.sync
        def _(sp):
            waits = []

            def copy_v(g):
                sp.dma_start(v_sb[:, :, P * g:P * (g + 1)], v_next[:, :, P * g:P * (g + 1)]) \
                  .then_inc(s[f"v_copied{g}"], 16)
                waits.append((f"v_copied{g}", 16))

            if front:
                sp.dma_start(x_sb[:, :, :], env["x_v"][nxt, :, :, :]).then_inc(s["x_loaded"], 16)
                waits.append(("x_loaded", 16))
            if attend:
                copy_group(sp, env, 1)
                waits.append(("group_copied1", STACK_DMAS))
                copy_v(1)
            if store:
                for h in range(2):
                    part = slice(T // 2 * h, T // 2 * (h + 1))
                    await_read(sp, "agg", part.stop - 2)
                    await_read(sp, "agg", part.stop - 1)
                    sp.dma_start(env["out_v"][b - 1, :, part, :], resid[:, part, :]).then_inc(s["tokens_out"], 16)
                    sp.dma_start(env["tok_v"][b - 1, :, part, :], resid[:, part, :]).then_inc(s["tokens_out"], 16)
                waits.append(("tokens_out", 64))
                await_read(sp, "gate")
                sp.dma_start(env["logits_d"][b - 1, :, :], logits_sb[:, :]).then_inc(s["logits_out"], 16)
                waits.append(("logits_out", 16))
            if front:
                if attend:
                    sp.wait_ge(s["weighed"], UNITS // 2)
                for h in range(2):
                    await_read(sp, "proj", 1, h)
                copy_group(sp, env, 0)
                waits.append(("group_copied0", STACK_DMAS))
                await_read(sp, "v", T // 2 - 1)
                copy_v(0)
                sp.wait_ge(s["shift_known"], 1)
            for name, value in waits:
                sp.wait_ge(s[name], value)

        @block.tensor
        def _(pe):
            def scores(u):
                g, qb, kt = u // (NQB * T), u // T % NQB, u % T
                if u == UNITS // 2:
                    pe.wait_ge(s["group_copied1"], STACK_DMAS)
                if u >= 2:
                    pe.wait_ge(s["exp_done"], u - 1)
                for r in range(HG):
                    last = pe.matmul(score_ps[u % 2][:, QB * r:QB * (r + 1)],
                                     key_stack[:, HG * g + r, P * kt:P * (kt + 1)],
                                     query_stack[:, HG * g + r, QB * qb:QB * (qb + 1)], start=True, stop=True)
                last.then_inc(s["scores_ready"], 1)

            def weigh(u):
                g, blk, kt = u // (NQB * T), u // T, u % T
                if u == UNITS // 2:
                    pe.wait_ge(s["v_copied1"], 16)
                if kt == 0 and blk >= 2:
                    pe.wait_ge(s["acc_copied"], blk - 1)
                pe.wait_ge(s["exp_done"], u + 1)
                acc, p = acc_ps[blk % 2], probs[:, u % 3, :]
                for r in range(HG):
                    last = pe.matmul(acc[DH * r:DH * (r + 1), 0:QB],
                                     v_sb[:, kt, P * g + DH * r:P * g + DH * (r + 1)],
                                     p[:, QB * r:QB * (r + 1)], start=kt == 0, stop=kt == T - 1,
                                     skip_group_check=True, tile_position=(0, DH * r))
                last.then_inc(s["weighed"], 1)

            def total(blk):
                pe.wait_ge(s["summed"], (T - 1) * (blk + 1))
                for r in range(HG):
                    last = pe.matmul(acc_ps[blk % 2][DH * r:DH * (r + 1), QB:2 * QB], ones[:, 0:DH],
                                     prob_sum[:, blk % 2, QB * r:QB * (r + 1)], start=False, stop=True,
                                     skip_group_check=True, tile_position=(0, DH * r))
                last.then_inc(s["blocks_done"], 1)

            def transposes(ps, *blocks):
                for j, m in enumerate(blocks):
                    last = pe.transpose(ps[:, P * j:P * (j + 1)], m, ident[:, :])
                return last

            def product(out, pairs):
                for j, (stationary, moving) in enumerate(pairs):
                    last = pe.matmul(out, stationary, moving, start=j == 0, stop=j == len(pairs) - 1)
                return last

            def step(st):
                kind, *at = st
                if kind in BANKLESS:
                    return
                ps, i, nth = bank(st)
                if nth:
                    pe.wait_ge(s[f"read{i}"], nth)
                tok = [slice(P * t, P * (t + 1)) for t in range(T)]
                half = [slice(P * c, P * (c + 1)) for c in range(CH)]
                if kind == "agg":
                    last = product(ps[:, 0:C], [(attn_T[:, c, tok[at[0]]], waggT[:, c, :]) for c in range(CH)])
                elif kind == "z2T":
                    pe.wait_ge(s["z2_ready"], 1)
                    last = transposes(ps, *(rows[:, at[0], half[c]] for c in range(CH)))
                elif kind == "gate":
                    for t in range(T - 2, T):
                        await_read(pe, "z2T", t)
                    for t in range(T):
                        last = product(ps[:, E * t:E * (t + 1)],
                                       [(chan[:, c, tok[t]], gate_w[:, c, :]) for c in range(CH)])
                elif kind == "xT":
                    c, h = at
                    pe.wait_ge(s["x_loaded"], 16)
                    last = transposes(ps, *(x_sb[:, 4 * h + j, half[c]] for j in range(4)))
                elif kind == "gmean":
                    pe.wait_ge(s["mean_ready"], 1)
                    last = product(ps[:, 0:CH], [(gn_mean[:, :], small[:, 0, :])])
                elif kind == "gvar":
                    pe.wait_ge(s["dev_ready"], 1)
                    last = product(ps[:, 0:CH], [(gn_mean[:, :], small[:, 3, :])])
                elif kind == "qk0":
                    pe.wait_ge(s["xn_ready"], 1)
                    last = product(ps[:, :], [(chan[:, c, tok[at[0]]], w0_sb[:, c, 0:2 * C]) for c in range(CH)])
                elif kind == "v0":
                    last = product(ps[:, 0:C],
                                   [(chan[:, c, tok[at[0]]], w0_sb[:, c, 2 * C:3 * C]) for c in range(CH)])
                elif kind == "sumv":
                    pe.wait_ge(s["x_sum_ready"], 1)
                    last = product(ps[:, 0:C], [(x_sum[:, c, :], w0_sb[:, c, 2 * C:3 * C]) for c in range(CH)])
                elif kind == "dots":
                    pe.wait_ge(s["head_scaled"], 2)
                    await_read(pe, "v0", T - 1)
                    for c in range(CH):
                        last = product(ps[:, half[c]], [(qk0[:, t, C + P * c:C + P * (c + 1)], rows[:, t, half[c]])
                                                        for t in range(T)])
                elif kind == "qT":
                    c, h = at
                    last = transposes(ps, *(qk0[:, 4 * h + j, half[c]] for j in range(4)))
                elif kind == "lin":
                    for h in range(2):
                        await_read(pe, "qT", CH - 1, h)
                    pe.wait_ge(s["dots_ready"], 1)
                    for c in range(CH):
                        last = product(ps[:, half[c]], [(qT[:, c, tok[at[0]]], dots_sb[:, c, :])])
                elif kind == "zT":
                    c, h = at
                    pe.wait_ge(s["z_ready"], 1)
                    last = transposes(ps, *(rows[:, 4 * h + j, half[c]] for j in range(4)))
                elif kind == "proj":
                    j, h = at
                    w = C * (j % 2) + P * (j // 2)
                    for hh_ in range(2):
                        await_read(pe, "zT", CH - 1, hh_)
                    last = product(ps[:, :], [(w1T[:, c, w:w + P], chan[:, c, BANK * h:BANK * (h + 1)])
                                              for c in range(CH)])
                elif kind == "v":
                    for j in range(2):
                        last = product(ps[:, C * j:C * (j + 1)],
                                       [(chan[:, c, tok[2 * at[0] + j]], w1T[:, c, 2 * C:3 * C]) for c in range(CH)])
                elif kind == "norms":
                    pe.wait_ge(s["norm_squared"], at[0] + 1)
                    last = product(ps[:, :], [(head_ones[:, :], norm_sq[:, :])])
                elif kind == "bound":
                    pe.wait_ge(s["bound_ready"], 1)
                    last = pe.transpose(ps[0:1, 0:P], bound[:, 0:1], ident[:, :])
                last.then_inc(s[f"full{i}"], 1)

            if attend:
                scores(0)
            for u, slot in enumerate(slots):
                if attend and u + 1 < UNITS:
                    scores(u + 1)
                for st in slot[:1]:
                    step(st)
                if attend and u:
                    weigh(u - 1)
                for st in slot[1:]:
                    step(st)
                if attend and u > T and u % T == 1:
                    total(u // T - 1)
            if attend:
                weigh(UNITS - 1)
                total(G * NQB - 1)

        @block.scalar
        def _(act):
            def step(st):
                kind, *at = st
                if kind == "z2T":
                    ps = await_full(act, *st)
                    read(act.activation(chan[:, :, P * at[0]:P * (at[0] + 1)],
                                        ps[:, 0:C].rearrange("p (c n) -> p c n", c=CH), ACT.Copy), *st)
                elif kind in ("xT", "zT"):
                    c, h = at
                    ps = await_full(act, *st)
                    read(act.activation(chan[:, c, BANK * h:BANK * (h + 1)], ps[:, :], ACT.Copy), *st)
                elif kind == "qk0":
                    if at[0] == 0 and attend:
                        act.wait_ge(s["group_copied1"], STACK_DMAS)
                    ps = await_full(act, *st)
                    read(act.activation(qk0[:, at[0], :], ps[:, :], ACT.Copy), *st)
                elif kind == "v0":
                    ps = await_full(act, *st)
                    read(act.activation(rows[:, at[0], :], ps[:, 0:C], ACT.Copy), *st)
                elif kind == "qT":
                    c, h = at
                    ps = await_full(act, *st)
                    read(act.activation(qT[:, c, BANK * h:BANK * (h + 1)], ps[:, :], ACT.Identity,
                                        bias=gb[:, 1:2], scale=gb[:, 0:1]), *st)
                elif kind == "proj":
                    j, h = at
                    ps = await_full(act, *st)
                    act.activation(hi[:, j, BANK * h:BANK * (h + 1)].bitcast(F32R), ps[:, :], ACT.Copy) \
                       .then_inc(s["hi_ready"], 1)
                elif kind == "v":
                    ps = await_full(act, *st)
                    if at[0] == 0 and attend:
                        act.wait_ge(s["v_copied1"], 16)
                    read(act.activation(v_next[:, 2 * at[0]:2 * at[0] + 2, :],
                                        ps[:, :].rearrange("p (t n) -> p t n", t=2), ACT.Copy), *st)

            def copy_acc(blk):
                act.wait_ge(s["blocks_done"], blk + 1)
                if blk:
                    act.wait_ge(s["attn_ready"], blk)
                act.activation(acc_sb[:, :], acc_ps[blk % 2][:, :], ACT.Copy) \
                   .then_inc(s["acc_copied"], 1)

            for u, slot in enumerate(slots):
                if attend:
                    act.wait_ge(s["scores_ready"], u + 1)
                    if u >= 3:
                        act.wait_ge(s["weighed"], u - 2)
                        act.wait_ge(s["summed"], (T - 1) * ((u - 3) // T) + max((u - 3) % T, 1))
                    act.activation(probs[:, u % 3, :], score_ps[u % 2][:, :], ACT.Exp, scale=DH ** -0.5) \
                       .then_inc(s["exp_done"], 1)
                for st in slot:
                    step(st)
                if attend and u > T and u % T == 2:
                    copy_acc(u // T - 1)
            if attend:
                copy_acc(G * NQB - 1)

        @block.gpsimd
        def _(pool):
            def divide(blk):
                g, qb = blk // NQB, blk % NQB
                pool.wait_ge(s["recip_ready"], blk + 1)
                pool.tensor_tensor(attn_T[:, g, QB * qb:QB * (qb + 1)], acc_sb[:, 0:QB],
                                   acc_sb[:, QB:2 * QB], ALU.mult).then_inc(s["attn_ready"], 1)

            def step(st):
                kind, *at = st
                if kind == "v0":
                    t = at[0]
                    await_read(pool, "qk0", t)
                    if t == 0 and attend:
                        pool.wait_ge(s["v_copied1"], 16)
                    if t >= 2:
                        pool.wait_ge(s["squares_summed"], t - 1)
                    pool.tensor_tensor(squares[:, t % 2, :], qk0[:, t, :], qk0[:, t, :], ALU.mult) \
                        .then_inc(s["squared"], 1)
                elif kind == "head_scale":
                    pool.wait_ge(s["head_r_ready"], at[0] + 1)
                    for t in range(T // 2 * at[0], T // 2 * (at[0] + 1)):
                        view = qk0[:, t, :].rearrange("p (h d) -> p h d", d=DH)
                        last = pool.tensor_tensor(
                            view, view, hr[:, t, :].unsqueeze(2).to_broadcast([P, 2 * H, DH]), ALU.mult)
                    last.then_inc(s["head_scaled"], 1)
                elif kind == "norms":
                    n = at[0]
                    part = hi[:, n // 2, BANK * (n % 2):BANK * (n % 2 + 1)]
                    await_read(pool, "proj", n // 2, n % 2)
                    if n:
                        await_read(pool, "norms", n - 1)
                    pool.tensor_tensor(norm_sq[:, :], part, part, ALU.mult).then_inc(s["norm_squared"], 1)

            for u, slot in enumerate(slots):
                if attend and u == T // 2:
                    if store:
                        pool.wait_ge(s["tokens_out"], 64)
                        pool.wait_ge(s["z2_ready"], 1)
                    for t in range(T):
                        pool.tensor_tensor(resid[:, t, :], lin_out[:, t, :], bias[:, :], ALU.add) \
                            .then_inc(s["resid_ready"], 1)
                for st in slot:
                    step(st)
                if attend and u > T and u % T == 4:
                    divide(u // T - 1)
            if attend:
                divide(G * NQB - 1)

        @block.vector
        def _(dve):
            link = Chain(dve, s["dve_done"])

            def layer_norm(src):
                link(dve.tensor_scalar(ln_v[:, :], mv[:, :, 1], LN_EPS, None, ALU.add))
                rsqrt(dve, link, ln_v[:, :], ln_r[:, :], ln_h[:, :])
                for t in range(T):
                    last = dve.tensor_scalar(rows[:, t, :], src[:, t, :], mv[:, t, 0:1], ln_r[:, t:t + 1],
                                             ALU.subtract, ALU.mult)
                return last

            def add_tokens(st, target, source):
                t = st[1]
                ps = await_full(dve, *st)
                read(dve.tensor_tensor(target[:, t, :], ps[:, 0:C], source[:, t, :], ALU.add), *st)
                await_read(dve, *st)
                link(dve.bn_stats(bn6[:, t, :], target[:, t, :]))
                link(dve.bn_aggr(mv[:, t, :], bn6[:, t, :]))

            def step(st):
                kind, *at = st
                if kind == "agg":
                    add_tokens(st, resid, resid)
                elif kind == "store_stats":
                    layer_norm(resid).then_inc(s["z2_ready"], 1)
                elif kind == "gate":
                    ps = await_full(dve, *st)
                    read(dve.tensor_scalar(logits_sb[:, :], ps[:, 0:T * E], CLIP, None, ALU.max), *st)
                elif kind == "xT":
                    c, h = at
                    await_read(dve, *st)
                    link(dve.bn_stats(bn6[:, 2 * c + h, :], chan[:, c, BANK * h:BANK * (h + 1)]))
                    if h:
                        link(dve.bn_aggr(mv[:, c, :], bn6[:, 2 * c:2 * c + 2, :].rearrange("p a b -> p (a b)")))
                    if st == LAST_X:
                        dve.tensor_copy(small[:, 0, :], mv[:, 0:CH, 0]).then_inc(s["mean_ready"], 1)
                elif kind == "gmean":
                    ps = await_full(dve, *st)
                    read(dve.tensor_copy(small[:, 1, :], ps[:, 0:CH]), *st)
                    await_read(dve, *st)
                    link(dve.tensor_tensor(small[:, 2, :], small[:, 0, :], small[:, 1, :], ALU.subtract))
                    link(dve.tensor_tensor(small[:, 3, :], small[:, 2, :], small[:, 2, :], ALU.mult))
                    dve.tensor_tensor(small[:, 3, :], small[:, 3, :], mv[:, 0:CH, 1], ALU.add) \
                       .then_inc(s["dev_ready"], 1)
                elif kind == "gvar":
                    ps = await_full(dve, *st)
                    read(dve.tensor_scalar(small[:, 4, :], ps[:, 0:CH], LN_EPS, None, ALU.add), *st)
                    await_read(dve, *st)
                    rsqrt(dve, link, small[:, 4, :], small[:, 5, :], small[:, 6, :])
                    for c in range(CH):
                        last = dve.tensor_scalar(chan[:, c, :], chan[:, c, :], small[:, 1, c:c + 1],
                                                 small[:, 5, c:c + 1], ALU.subtract, ALU.mult)
                    last.then_inc(s["xn_ready"], 1)
                    link(dve.scalar_tensor_tensor(out=small[:, 7, :], in0=small[:, 2, :], scalar=float(N),
                                                  in1=small[:, 5, :], op0=ALU.mult, op1=ALU.mult))
                    for c in range(CH):
                        last = dve.tensor_scalar(x_sum[:, c, :], ones[:, :], small[:, 7, c:c + 1], None, ALU.mult)
                    last.then_inc(s["x_sum_ready"], 1)
                elif kind == "v0":
                    t = at[0]
                    dve.wait_ge(s["squared"], t + 1)
                    dve.tensor_reduce(ss[:, t, :], squares[:, t % 2, :].rearrange("p (h d) -> p h d", d=DH),
                                      AX.X, ALU.add).then_inc(s["squares_summed"], 1)
                elif kind == "head_scale":
                    part = slice(T // 2 * at[0], T // 2 * (at[0] + 1))
                    dve.wait_ge(s["squares_summed"], part.stop)
                    flat = [m[:, part, :].rearrange("p t h -> p (t h)") for m in (ss, hr, hh)]
                    link(dve.tensor_scalar(flat[0], flat[0], 1.0 / DH, LN_EPS, ALU.mult, ALU.add))
                    rsqrt(dve, link, *flat)
                    dve.wait_ge(s["squares_summed"], part.stop)
                    dve.sem_inc(s["head_r_ready"], 1)
                elif kind == "sumv":
                    ps = await_full(dve, *st)
                    read(dve.tensor_scalar(sumv_sb[:, :], ps[:, 0:C], gb[:, 3:4], None, ALU.mult), *st)
                elif kind == "dots":
                    await_read(dve, "sumv")
                    ps = await_full(dve, *st)
                    flat = dots_sb[:, :, :].rearrange("p c n -> p (c n)")
                    read(dve.scalar_tensor_tensor(out=flat, in0=ps[:, 0:C], scalar=gb[:, 2:3], in1=sumv_sb[:, :],
                                                  op0=ALU.mult, op1=ALU.add), *st)
                    await_read(dve, *st)
                    dve.tensor_tensor(flat, flat, head_mask[:, :, :].rearrange("p c n -> p (c n)"), ALU.mult) \
                       .then_inc(s["dots_ready"], 1)
                elif kind == "lin":
                    if at[0] == 0 and attend:
                        dve.wait_ge(s["resid_ready"], T)
                    add_tokens(st, lin_out, x_sb)
                elif kind == "front_stats":
                    layer_norm(lin_out).then_inc(s["z_ready"], 1)
                elif kind == "proj":
                    j, h = at
                    part = slice(BANK * h, BANK * (h + 1))
                    ps = await_full(dve, *st)
                    dve.wait_ge(s["hi_ready"], 2 * j + h + 1)
                    read(dve.tensor_tensor(lo[:, j, part].bitcast(F32R), ps[:, :], hi[:, j, part], ALU.subtract), *st)
                elif kind == "norms":
                    n = at[0]
                    ps = await_full(dve, *st)
                    read(dve.tensor_reduce(norm_max[:, n // 2, n % 2:n % 2 + 1], ps[:, :], AX.X, ALU.max), *st)
                    if n < 7:
                        return
                    await_read(dve, *st)
                    link(dve.tensor_reduce(bound[:, 1:5], norm_max[:, :, :], AX.X, ALU.max))
                    for g in range(G):
                        link(dve.tensor_tensor(bound[:, 5 + g:6 + g], bound[:, 1 + 2 * g:2 + 2 * g],
                                               bound[:, 2 + 2 * g:3 + 2 * g], ALU.mult))
                    dve.tensor_tensor(bound[:, 0:1], bound[:, 5:6], bound[:, 6:7], ALU.max) \
                       .then_inc(s["bound_ready"], 1)
                elif kind == "bound":
                    ps = await_full(dve, *st)
                    read(dve.tensor_reduce(bound[0:1, 7:8], ps[0:1, 0:P], AX.X, ALU.max), *st)
                    await_read(dve, *st)
                    dve.tensor_scalar(shifted[:, :], bound[0:1, 7:8], 0.99 * DH * SAFE_SCORE ** 2, None,
                                      ALU.is_gt).then_inc(s["shift_known"], 1)

            def invert(blk):
                dve.wait_ge(s["acc_copied"], blk + 1)
                dve.reciprocal(acc_sb[:, QB:2 * QB], acc_sb[:, QB:2 * QB]).then_inc(s["recip_ready"], 1)

            def add_up(u):
                kt, total = u % T, prob_sum[:, u // T % 2, :]
                if not kt:
                    return
                dve.wait_ge(s["exp_done"], u + 1)
                if kt == 1 and u > 2 * T:
                    dve.wait_ge(s["blocks_done"], u // T - 1)
                if kt > 1:
                    dve.wait_ge(s["summed"], (T - 1) * (u // T) + kt - 1)
                dve.tensor_tensor(total, probs[:, (u - 1) % 3, :] if kt == 1 else total, probs[:, u % 3, :],
                                  ALU.add).then_inc(s["summed"], 1)

            for u, slot in enumerate(slots):
                if attend and u:
                    add_up(u - 1)
                for st in slot:
                    step(st)
                if attend and u > T and u % T == 3:
                    invert(u // T - 1)
            if attend:
                add_up(UNITS - 1)
                invert(G * NQB - 1)


def build_experts(nc, ctx, env):
    def sb(name, shape, dt=F32):
        return ctx.enter_context(nc.sbuf_tensor(name, shape, dt))

    def ps(name, shape):
        return ctx.enter_context(nc.psum_tensor(name, shape, F32))

    ident, ones = env["ident"], env["ones"]
    tokens, out_rows = env["tokens"], env["out_rows"]
    BE = B * E
    gates = sb("gates", [P, B, T, E])
    gates_t = sb("gates_t", [P, T, B, E])
    col = sb("col", [P, B, E])
    col_r = sb("col_r", [P, B, E])
    row = sb("row", [P, B * T])
    row_r = sb("row_r", [P, B * T])
    work = sb("work", [BE, 2, N])
    best = sb("best", [BE, M])
    best_i = sb("best_i", [BE, M], U32)
    best_f = sb("best_f", [BE, M])
    first_token = sb("first_token", [P, B], I32)
    first_token_f = sb("first_token_f", [P, B])
    slot_token = sb("slot_token", [P, E, B], U32)
    slot_gate = sb("slot_gate", [P, E, B])
    w_sb = sb("w_sb", [P, E, CH, C])
    picked = sb("picked", [P, 2, B, C])
    z = sb("z", [P, 2, B, C])
    zT = sb("zT3", [P, 2, CH, P])
    result = sb("result", [P, 2, B, C])
    bn6 = sb("bn6e", [P, B, 6])
    mv = sb("mve", [P, B, 2])
    ln_v, ln_r, ln_h = sb("ln_ve", [P, B]), sb("ln_re", [P, B]), sb("ln_he", [P, B])
    sum_ps = ps("sum_ps", [P, BANK])
    wide_ps = ps("wide_ps", [P, 2 * BANK])
    zT_ps = [ps(f"zT_ps{i}", [P, BANK]) for i in range(2)]
    y_ps = [ps(f"y_ps{i}", [P, BANK]) for i in range(2)]
    names = ("logits_in w_in dve_done sums_ready gates_ready turned gates_copied lists_ready lists_turned "
             "iota_done chosen z_ready zT_ready zT_read y_ready result_ready").split()
    s = {n: ctx.enter_context(nc.semaphore(n + "_e")) for n in names}
    s["scattered"] = ctx.enter_context(nc.semaphore("scattered"))
    s["picked_in"] = [ctx.enter_context(nc.semaphore(f"picked_in{i}")) for i in range(2)]

    def gather(pool, e, b):
        pool.indirect_dma_start(picked[:, e % 2, b, :], None, tokens[:, :],
                                bass.IndirectOffsetOnAxis(ap=slot_token[:, e, b:b + 1], axis=0)) \
            .then_inc(s["picked_in"][e % 2], 16)

    with nc.Block() as block:
        @block.sync
        def _(sp):
            sp.dma_start(gates[:, :, :, :].rearrange("p b t e -> p b (t e)"),
                         env["logits_d"].rearrange("b p n -> p b n")).then_inc(s["logits_in"], 16)
            sp.dma_start(w_sb[:, :, :, :], env["wexp"].rearrange("e (c p) o -> p e c o", p=P)).then_inc(s["w_in"], 16)
            sp.wait_ge(s["w_in"], 16)

        @block.tensor
        def _(pe):
            pe.wait_ge(s["logits_in"], 16)
            for it in range(SINKHORN_ITERS):
                if it:
                    pe.wait_ge(s["gates_ready"], it)
                pe.matmul(sum_ps[:, :], ones[:, :], gates[:, :, :, :].rearrange("p b t e -> p (b t e)"),
                          start=True, stop=True).then_inc(s["sums_ready"], 1)
            pe.wait_ge(s["gates_ready"], SINKHORN_ITERS)
            for t in range(T):
                last = pe.transpose(wide_ps[0:BE, P * t:P * (t + 1)],
                                    gates_t[:, t, :, :].rearrange("p b e -> p (b e)"), ident[:, :])
            last.then_inc(s["turned"], 1)
            pe.wait_ge(s["lists_ready"], 2)
            pe.transpose(zT_ps[0][:, 0:BE], best_f[:, :], ident[0:BE, 0:BE])
            pe.transpose(zT_ps[1][:, 0:BE], best[:, :], ident[0:BE, 0:BE]).then_inc(s["lists_turned"], 1)
            pe.wait_ge(s["chosen"], 1)
            pe.wait_ge(s["w_in"], 16)

            def turn(n):
                pe.wait_ge(s["z_ready"], n + 1)
                if n >= 2:
                    pe.wait_ge(s["zT_read"], n - 1)
                for c in range(CH):
                    last = pe.transpose(zT_ps[n % 2][:, P * c:P * (c + 1)], z[:, n // B % 2, n % B, P * c:P * (c + 1)],
                                        ident[:, :])
                last.then_inc(s["zT_ready"], 1)

            def multiply(n):
                pe.wait_ge(s["zT_read"], n + 1)
                if n >= 2:
                    pe.wait_ge(s["result_ready"], n - 1)
                for c in range(CH):
                    last = pe.matmul(y_ps[n % 2][:, 0:C], zT[:, n % 2, c, :], w_sb[:, n // B, c, :],
                                     start=c == 0, stop=c == CH - 1)
                last.then_inc(s["y_ready"], 1)

            turn(0)
            for n in range(E * B):
                if n + 1 < E * B:
                    turn(n + 1)
                multiply(n)

        @block.gpsimd
        def _(pool):
            pool.iota(first_token[:, :], pattern=[[N, B]], base=0, channel_multiplier=0).then_inc(s["iota_done"], 1)
            pool.wait_ge(s["chosen"], 1)
            for e in range(2):
                for b in range(B):
                    gather(pool, e, b)
            for e in range(E):
                if e:
                    pool.wait_ge(s["scattered"], 16 * B * e)
                for b in range(B):
                    pool.wait_ge(s["result_ready"], B * e + b + 1)
                    pool.indirect_dma_start(out_rows[:, :],
                                            bass.IndirectOffsetOnAxis(ap=slot_token[:, e, b:b + 1], axis=0),
                                            result[:, e % 2, b, :], None).then_inc(s["scattered"], 16)
                if e + 2 < E:
                    for b in range(B):
                        gather(pool, e + 2, b)
            pool.wait_ge(s["scattered"], 16 * B * E)

        @block.vector
        def _(dve):
            link = Chain(dve, s["dve_done"])
            flat = gates[:, :, :, :].rearrange("p b t e -> p (b t e)")
            by_token = gates[:, :, :, :].rearrange("p b t e -> p (b t) e")
            dve.wait_ge(s["logits_in"], 16)
            for it in range(SINKHORN_ITERS):
                dve.wait_ge(s["sums_ready"], it + 1)
                link(dve.tensor_reduce(col[:, :, :], sum_ps[:, :].rearrange("p (b t e) -> p b e t", b=B, t=T),
                                       AX.X, ALU.add))
                link(dve.reciprocal(col_r[:, :, :], col[:, :, :]))
                link(dve.tensor_tensor(gates[:, :, :, :], gates[:, :, :, :],
                                       col_r[:, :, :].unsqueeze(2).to_broadcast([P, B, T, E]), ALU.mult))
                link(dve.tensor_reduce(row[:, :], by_token, AX.X, ALU.add))
                link(dve.reciprocal(row_r[:, :], row[:, :]))
                if it < SINKHORN_ITERS - 1:
                    dve.tensor_tensor(by_token, by_token, row_r[:, :].unsqueeze(2).to_broadcast([P, B * T, E]),
                                      ALU.mult).then_inc(s["gates_ready"], 1)
                else:
                    dve.tensor_tensor(gates_t[:, :, :, :].rearrange("p t b e -> p b t e"), gates[:, :, :, :],
                                      row_r[:, :].rearrange("p (b t) -> p b t", b=B).unsqueeze(3)
                                      .to_broadcast([P, B, T, E]), ALU.mult).then_inc(s["gates_ready"], 1)
                dve.wait_ge(s["gates_ready"], it + 1)
            dve.wait_ge(s["turned"], 1)
            link(dve.tensor_copy(work[:, 0, :], wide_ps[0:BE, :]))
            for r in range(M // 8):
                eight = slice(8 * r, 8 * (r + 1))
                src, dst = work[:, r % 2, :], work[:, (r + 1) % 2, :]
                link(dve.max(best[:, eight], src))
                link(dve.max_index(best_i[:, eight], best[:, eight], src))
                if r < M // 8 - 1:
                    link(dve.match_replace(dst, best[:, eight], src, -1.0))
            dve.sem_inc(s["lists_ready"], 1)
            dve.tensor_copy(best_f[:, :], best_i[:, :]).then_inc(s["lists_ready"], 1)
            dve.wait_ge(s["iota_done"], 1)
            link(dve.tensor_copy(first_token_f[:, :], first_token[:, :]))
            dve.wait_ge(s["lists_turned"], 1)
            link(dve.tensor_tensor(slot_token[:, 0:E, :].rearrange("p e b -> p b e"),
                                   zT_ps[0][:, 0:BE].rearrange("p (b e) -> p b e", b=B),
                                   first_token_f[:, :].unsqueeze(2).to_broadcast([P, B, E]), ALU.add))
            link(dve.tensor_copy(slot_gate[:, :, :].rearrange("p e b -> p b e"),
                                 zT_ps[1][:, 0:BE].rearrange("p (b e) -> p b e", b=B)))
            dve.sem_inc(s["chosen"], 1)

            def normalise(e):
                dve.wait_ge(s["picked_in"][e % 2], 16 * B * (e // 2 + 1))
                for b in range(B):
                    link(dve.bn_stats(bn6[:, b, :], picked[:, e % 2, b, :]))
                    link(dve.bn_aggr(mv[:, b, :], bn6[:, b, :]))
                link(dve.tensor_scalar(ln_v[:, :], mv[:, :, 1], LN_EPS, None, ALU.add))
                rsqrt(dve, link, ln_v[:, :], ln_r[:, :], ln_h[:, :])
                if e >= 2:
                    dve.wait_ge(s["zT_ready"], B * (e - 1))
                for b in range(B):
                    dve.tensor_scalar(z[:, e % 2, b, :], picked[:, e % 2, b, :], mv[:, b, 0:1], ln_r[:, b:b + 1],
                                      ALU.subtract, ALU.mult).then_inc(s["z_ready"], 1)

            normalise(0)
            for e in range(E):
                if e + 1 < E:
                    normalise(e + 1)
                if e >= 2:
                    dve.wait_ge(s["scattered"], 16 * B * (e - 1))
                for b in range(B):
                    n = B * e + b
                    dve.wait_ge(s["y_ready"], n + 1)
                    dve.scalar_tensor_tensor(out=result[:, e % 2, b, :], in0=y_ps[n % 2][:, 0:C],
                                             scalar=slot_gate[:, e, b:b + 1], in1=picked[:, e % 2, b, :],
                                             op0=ALU.mult, op1=ALU.add).then_inc(s["result_ready"], 1)

        @block.scalar
        def _(act):
            for n in range(E * B):
                act.wait_ge(s["zT_ready"], n + 1)
                if n >= 2:
                    act.wait_ge(s["y_ready"], n - 1)
                act.activation(zT[:, n % 2, :, :].rearrange("p c n -> p (c n)"), zT_ps[n % 2][:, 0:C], ACT.Copy) \
                   .then_inc(s["zT_read"], 1)


_INS = ['x', 'L0_conv_w_qkv', 'L0_conv_q_gamma', 'L0_conv_q_beta', 'L0_conv_k_gamma', 'L0_conv_k_beta',
        'L1_attn_w_qkv', 'L1_attn_w_agg', 'L1_attn_b_agg', 'L1_ffn_gate_weight', 'L1_ffn_experts']
_OUTS = [((8, 32, 32, 256), 'float32')]


def kernel(**inputs):
    import numpy as _np
    import concourse.bacc as _bacc
    from concourse import mybir as _mybir
    from concourse.bass_utils import run_bass_kernel_spmd as _run

    nc = _bacc.Bacc("TRN2", target_bir_lowering=False, num_devices=1)
    arrays, args = {}, []
    for name in _INS:
        a = _np.ascontiguousarray(inputs[name])
        arrays[f"in_{name}_dram"] = a
        args.append(nc.dram_tensor(f"in_{name}_dram", a.shape, _mybir.dt.from_np(a.dtype), kind="ExternalInput").ap())
    for i, (shape, dtype) in enumerate(_OUTS):
        dt = _mybir.dt.from_np(_np.dtype(dtype))
        args.append(nc.dram_tensor(f"out_{i}_dram", shape, dt, kind="ExternalOutput").ap())
    hybrid_kernel(nc, *args)
    r = _run(nc, [arrays], core_ids=[0])
    return r.results[0]["out_0_dram"]
```

```python
import numpy as np
import concourse.bass as bass
from concourse import mybir
from contextlib import ExitStack

F32 = mybir.dt.float32
F32R = mybir.dt.float32r
I32 = mybir.dt.int32
U32 = mybir.dt.uint32
ALU = mybir.AluOpType
ACT = mybir.ActivationFunctionType
AX = mybir.AxisListType

P = 128
B = 8
N = 1024
C = 256
T = N // P
CH = C // P
H = 8
DH = C // H
HG = P // DH
G = H // HG
E = 8
M = N // E
GROUP = C // 32
BANK = 512
QB = 256
NQB = N // QB
BLOCK_UNITS = T
UNITS = G * NQB * BLOCK_UNITS
SINKHORN_ITERS = 8
LN_EPS = 1e-5
CLIP = 1e-6
PICKED = 3
DIRECT = 1
DIRECT_ALONE = 1
MAX_ROW = 3 * DH
RSQRT_SEED = 0x5F3759DF
SAFE_SCORE = 64.0


def spread(steps, slots):
    rests = sum(x[1] for x in steps if x[0] == "rest")
    share = sum(WORK[x[0]] for x in steps if x[0] != "rest") / (slots - rests)
    done, out = 0.0, [[] for _ in range(slots)]
    for x in steps:
        if x[0] == "rest":
            done += x[1]
        else:
            out[min(int(done + 1e-6), slots - 1)].append(x)
            done += WORK[x[0]] / share
    return out


def order(attend, front, store):
    store_part = {"agg", "store_stats", "store_rows", "z2T", "gate"}
    attend_part = {"resid"}
    steps = [("agg", 0), ("agg", 1), ("agg", 2), ("agg", 3), ("xT", 0, 0), ("xT", 0, 1), ("rest", 0.5),
             ("store_stats", 0), ("xT", 1, 0), ("agg", 4), ("xT", 1, 1), ("agg", 5), ("x_stats",), ("agg", 6),
             ("gmean",), ("agg", 7), ("store_rows", 0), ("gvar",), ("store_rows", 1), ("store_stats", 1),
             ("z2T", 0), ("store_rows", 2), ("z2T", 1), ("store_rows", 3), ("z2T", 2), ("rest", 1), ("z2T", 3),
             ("gate", 0), ("rest", 1), ("xn", 0), ("xn", 1), ("rest", 2), ("qk0", 0), ("store_rows", 4),
             ("gate", 1), ("z2T", 4), ("v0", 0), ("store_rows", 5), ("qk0", 1), ("gate", 2), ("store_rows", 6),
             ("gate", 3), ("v0", 1), ("store_rows", 7), ("z2T", 5), ("z2T", 6), ("gate", 4), ("qk0", 2), ("z2T", 7),
             ("gate", 5), ("x_sum",), ("v0", 2), ("gate", 6), ("resid", 0), ("qk0", 3), ("gate", 7), ("resid", 1),
             ("v0", 3), ("head_stats", 0), ("qk0", 4), ("v0", 4), ("resid", 2), ("qk0", 5), ("resid", 3), ("v0", 5),
             ("qk0", 6), ("resid", 4), ("v0", 6), ("qk0", 7), ("head_scale", 0), ("resid", 5), ("v0", 7),
             ("head_scale", 1), ("head_stats", 1), ("rest", 1), ("resid", 6), ("resid", 7), ("sumv",), ("qT", 0, 0),
             ("qT", 1, 0), ("head_scale", 2), ("head_scale", 3), ("rest", 3), ("qT", 0, 1), ("qT", 1, 1), ("dots",),
             ("rest", 1), ("lin", 0), ("lin", 1), ("lin", 2), ("lin", 3), ("front_stats", 0), ("lin", 4),
             ("lin", 5), ("lin", 6), ("lin", 7), ("rest", 1), ("front_stats", 1), ("front_rows", 0),
             ("front_rows", 1), ("front_rows", 2), ("rest", 1), ("front_rows", 3), ("rest", 1), ("zT", 0, 0),
             ("zT", 1, 0), ("proj", 0, 0), ("front_rows", 4), ("front_rows", 5), ("proj", 1, 0), ("square", 0, 0),
             ("proj", 2, 0), ("front_rows", 6), ("norms", 0, 0), ("square", 1, 0), ("proj", 3, 0),
             ("front_rows", 7), ("norms", 1, 0), ("square", 2, 0), ("zT", 0, 1), ("zT", 1, 1), ("norms", 2, 0),
             ("square", 3, 0), ("proj", 0, 1), ("proj", 1, 1), ("norms", 3, 0), ("square", 0, 1), ("v", 0),
             ("norms", 0, 1), ("square", 1, 1), ("v", 1), ("norms", 1, 1), ("proj", 2, 1), ("v", 2),
             ("square", 2, 1), ("proj", 3, 1), ("norms", 2, 1), ("square", 3, 1), ("v", 3), ("norms", 3, 1),
             ("rest", 2), ("bound_rows",), ("rest", 2), ("bound",), ("rest", 2)]
    wanted = {"store": store, "attend": attend, "front": front, "rest": attend and front}
    part = {k: "store" for k in store_part} | {k: "attend" for k in attend_part} | {"rest": "rest"}
    return [x for x in steps if wanted[part.get(x[0], "front")]]


WORK = {"agg": 1.1, "store_stats": 0.5, "store_rows": 0.22, "z2T": 0.4, "gate": 0.4, "xT": 0.6, "x_stats": 0.4,
        "gmean": 0.3, "gvar": 0.21, "xn": 0.8, "x_sum": 0.2, "resid": 0.0, "qk0": 1.8, "v0": 0.9,
        "head_stats": 0.28, "head_scale": 0.8, "sumv": 0.9, "dots": 3.5, "qT": 0.5, "lin": 1.1, "front_stats": 0.5,
        "front_rows": 0.1, "zT": 0.9, "proj": 1.8, "v": 1.8, "square": 0, "norms": 0.5, "bound_rows": 0.5,
        "bound": 0.3}
BANKLESS = {"store_stats", "store_rows", "front_stats", "front_rows", "x_stats", "xn", "x_sum", "resid", "head_stats",
            "head_scale", "square", "bound_rows"}


def bank_uses(slots):
    return {s: k for k, s in enumerate(s for slot in slots for s in slot if s[0] not in BANKLESS)}


def hybrid_kernel(nc, x, w0, q_gamma, q_beta, k_gamma, k_beta, w1, wagg, bagg, wgate, wexp, out):
    tokens = nc.dram_tensor("tokens_scratch", (B * N, C), F32).ap()
    logits_d = nc.dram_tensor("logits_scratch", (B, P, T * E), F32).ap()
    x_v = x.rearrange("b h w c -> b (h w) c").rearrange("b (t p) c -> b p t c", p=P)
    out_v = out.rearrange("b h w c -> b (h w) c").rearrange("b (t p) c -> b p t c", p=P)
    out_rows = out.rearrange("b h w c -> (b h w) c")
    tok_v = tokens.rearrange("(b t p) c -> b p t c", p=P, t=T)

    with ExitStack() as ctx:
        def sb(name, shape, dt=F32):
            return ctx.enter_context(nc.sbuf_tensor(name, shape, dt))

        ident = sb("ident", [P, P])
        ones = sb("ones", [P, P])
        gn_mean = sb("gn_mean", [P, P])
        head_mask = sb("head_mask", [P, CH, P])
        w0_sb = sb("w0_sb", [P, CH, 3 * C])
        w1T = sb("w1T", [P, CH, 3 * C])
        waggT = sb("waggT", [P, CH, C])
        bias = sb("bias", [P, C])
        gate_w = sb("gate_w", [P, CH, E])
        gb = sb("gb", [P, 4])

        x_sb = sb("x_sb", [P, T, C])

        setup_sems = ExitStack()
        with setup_sems:
            build_setup(nc, locals())

        phase = ExitStack()
        with phase:
            build_attention(nc, phase, locals())
        phase = ExitStack()
        with phase:
            build_experts(nc, phase, locals())


def build_setup(nc, env):
    ident, ones, gn_mean, head_mask = env["ident"], env["ones"], env["gn_mean"], env["head_mask"]
    w0_sb, w1T, waggT, bias, gate_w, gb = (env[k] for k in ("w0_sb", "w1T", "waggT", "bias", "gate_w", "gb"))
    with ExitStack() as ctx:
        def sem(name):
            return ctx.enter_context(nc.semaphore(name))

        w1_nat = ctx.enter_context(nc.sbuf_tensor("w1_nat", [P, 6, C], F32))
        wagg_nat = ctx.enter_context(nc.sbuf_tensor("wagg_nat", [P, CH, C], F32))
        bagg_row = ctx.enter_context(nc.sbuf_tensor("bagg_row", [1, C], F32))
        head_sum = ctx.enter_context(nc.sbuf_tensor("head_sum", [P, CH, 2 * H], F32))
        turned = [ctx.enter_context(nc.psum_tensor(f"turned{i}", [P, BANK], F32)) for i in range(5)]
        filled, constants, x_in, bias_in = sem("filled"), sem("constants"), sem("x_in"), sem("bias_in")
        to_turn_in, w0_in, small_in = sem("to_turn_in"), sem("w0_in"), sem("small_in")
        turned_ready, dve_chain = sem("turned_ready"), sem("dve_chain")
        block = ctx.enter_context(nc.Block())

        @block.sync
        def _(sp):
            sp.dma_start(w1_nat[:, :, :], env["w1"].rearrange("(c p) n -> p c n", p=P)).then_inc(to_turn_in, 16)
            sp.dma_start(wagg_nat[:, :, :], env["wagg"].rearrange("(c p) n -> p c n", p=P)).then_inc(to_turn_in, 16)
            sp.dma_start(w0_sb[:, :, :], env["w0"].rearrange("(c p) n -> p c n", p=P)).then_inc(w0_in, 16)
            sp.dma_start(env["x_sb"][:, :, :], env["x_v"][0, :, :, :]).then_inc(x_in, 16)
            sp.wait_ge(x_in, 16)

        @block.scalar
        def _(act):
            act.dma_start(bagg_row[:, :], env["bagg"].rearrange("(a n) -> a n", a=1)).then_inc(bias_in, 16)
            act.dma_start(gate_w[:, :, :], env["wgate"][0, :, :].rearrange("(c p) n -> p c n", p=P)).then_inc(small_in, 16)
            for col, v in enumerate(("q_gamma", "q_beta", "k_gamma", "k_beta")):
                for r in range(HG):
                    act.dma_start(gb[DH * r:DH * (r + 1), col:col + 1],
                                  env[v].rearrange("(n a) -> n a", a=1)).then_inc(small_in, 16)
            act.wait_ge(small_in, 16 * (1 + 4 * HG))

        @block.gpsimd
        def _(pool):
            pool.memset(ident[:, :], 0.0).then_inc(filled, 1)
            pool.memset(ones[:, :], 1.0).then_inc(filled, 1)
            pool.memset(gn_mean[:, :], 1.0 / GROUP).then_inc(filled, 1)
            pool.memset(head_mask[:, :, :], 1.0 / N).then_inc(filled, 1)
            pool.wait_ge(filled, 4)
            pool.affine_select(out=ident[:, :], in_=ident[:, :], compare_op=ALU.not_equal, fill=1.0,
                               base=0, pattern=[[-1, P]], channel_multiplier=1).then_inc(constants, 1)
            for n, (mat, width) in enumerate(((gn_mean[:, :], GROUP), (head_mask[:, :, :], DH))):
                blocks = P // width
                reps = [[0, CH]] if n else []
                view = mat.rearrange("p (g w) -> p g w", w=width) if not n else \
                    mat.rearrange("p c (g w) -> p c g w", w=width)
                pool.affine_select(out=view, in_=view, compare_op=ALU.is_ge, fill=0.0, base=0,
                                   pattern=[*reps, [-width, blocks], [0, width]],
                                   channel_multiplier=1).then_inc(constants, 1)
                pool.wait_ge(constants, 2 + 2 * n)
                pool.affine_select(out=view, in_=view, compare_op=ALU.is_ge, fill=0.0, base=width - 1,
                                   pattern=[*reps, [width, blocks], [0, width]],
                                   channel_multiplier=-1).then_inc(constants, 1)
            pool.wait_ge(constants, 5)

        @block.tensor
        def _(pe):
            pe.wait_ge(to_turn_in, 32)
            pe.wait_ge(constants, 5)
            for c in range(CH):
                for o in range(6):
                    pe.transpose(turned[2 * c + o // 4][:, P * (o % 4):P * (o % 4 + 1)],
                                 w1_nat[:, o, P * c:P * (c + 1)], ident[:, :])
            for c in range(CH):
                for o in range(CH):
                    pe.transpose(turned[2 * c + 1][:, 2 * P + P * o:3 * P + P * o],
                                 wagg_nat[:, o, P * c:P * (c + 1)], ident[:, :])
            pe.wait_ge(bias_in, 16)
            pe.matmul(turned[4][:, 0:C], ones[0:1, :], bagg_row[0:1, :], start=True, stop=True) \
              .then_inc(turned_ready, 1)

        @block.vector
        def _(dve):
            dve.wait_ge(w0_in, 16)
            qk = w0_sb[:, :, 0:2 * C].rearrange("p c (h d) -> p c h d", d=DH)
            for c in range(CH):
                dve.tensor_reduce(head_sum[:, c, :], qk[:, c], AX.X, ALU.add).then_inc(dve_chain, 1)
            dve.wait_ge(dve_chain, 2)
            dve.tensor_scalar(head_sum[:, :, :], head_sum[:, :, :], 1.0 / DH, None, ALU.mult).then_inc(dve_chain, 1)
            dve.wait_ge(dve_chain, 3)
            for c in range(CH):
                dve.tensor_tensor(qk[:, c], qk[:, c], head_sum[:, c, :].unsqueeze(2).to_broadcast([P, 2 * H, DH]),
                                  ALU.subtract).then_inc(dve_chain, 1)
            dve.wait_ge(turned_ready, 1)
            for c in range(CH):
                dve.tensor_copy(w1T[:, c, 0:BANK], turned[2 * c][:, :]).then_inc(dve_chain, 1)
                dve.tensor_copy(w1T[:, c, BANK:3 * C], turned[2 * c + 1][:, 0:C]).then_inc(dve_chain, 1)
                dve.tensor_copy(waggT[:, c, :], turned[2 * c + 1][:, C:2 * C]).then_inc(dve_chain, 1)
            dve.tensor_copy(bias[:, :], turned[4][:, 0:C]).then_inc(dve_chain, 1)
            dve.wait_ge(dve_chain, 12)


def newton_rsqrt(dve, link, v, y, half):
    link(dve.tensor_scalar(y.bitcast(I32), v.bitcast(I32), -0.5, float(RSQRT_SEED), ALU.mult, ALU.add))
    for _ in range(3):
        link(dve.scalar_tensor_tensor(out=half, in0=y, scalar=-0.5, in1=y, op0=ALU.mult, op1=ALU.mult))
        link(dve.tensor_tensor(half, half, v, ALU.mult))
        link(dve.scalar_tensor_tensor(out=y, in0=half, scalar=1.5, in1=y, op0=ALU.add, op1=ALU.mult))


class Chain:

    def __init__(self, engine, done):
        self.engine, self.done, self.count = engine, done, 0

    def __call__(self, instruction):
        instruction.then_inc(self.done, 1)
        self.count += 1
        self.engine.wait_ge(self.done, self.count)


def rsqrt(pool, link, v, y, half):
    link(pool.tensor_scalar(y.bitcast(I32), v.bitcast(I32), -0.5, float(RSQRT_SEED), ALU.mult, ALU.add))
    for _ in range(3):
        link(pool.tensor_tensor(half, y, y, ALU.mult))
        link(pool.tensor_tensor(half, half, v, ALU.mult))
        link(pool.tensor_scalar(half, half, -0.5, 1.5, ALU.mult, ALU.add))
        link(pool.tensor_tensor(y, y, half, ALU.mult))


def build_attention(nc, ctx, env):
    def sb(name, shape, dt=F32):
        return ctx.enter_context(nc.sbuf_tensor(name, shape, dt))

    key_stack = sb("key_stack", [P, H, N], F32R)
    query_stack = sb("query_stack", [P, H, N], F32R)
    hi = sb("hi", [P, 4, N])
    lo = sb("lo", [P, 4, N])
    v_sb = sb("v_sb", [P, T, C])
    v_next = sb("v_next", [P, T, C])
    x_sb = env["x_sb"]
    chan = sb("chan", [P, CH, N])
    rows = sb("rows", [P, T, C])
    lin_out = sb("lin_out", [P, T, C])
    resid = sb("resid", [P, T, C])
    attn_T = sb("attn_T", [P, G, N])
    probs = sb("probs", [P, 3, HG * QB])
    prob_sum = sb("prob_sum", [P, 2, HG * QB])
    acc_sb = sb("acc_sb", [P, BANK])
    head_ones = sb("head_ones", [P, P], F32R)
    norm_sq = sb("norm_sq", [P, BANK], F32R)
    norm_max = sb("norm_max", [P, 4, 2])
    bound = sb("bound", [P, 8])
    shifted = sb("shifted", [1, 1], I32)
    squares = v_next[:, 0:4, :].rearrange("p (i a) n -> p i (a n)", i=2)
    qT = hi[:, 0:2, :]
    z2T = hi[:, 2:4, :]
    qk0 = lo[:, :, :].rearrange("p j n -> p (j n)").rearrange("p (t n) -> p t n", n=2 * C)
    dots_sb = sb("dots_sb", [P, CH, P])
    sumv_sb = sb("sumv_sb", [P, C])
    x_sum = sb("x_sum", [P, CH, P])
    bn6 = sb("bn6", [P, T, 6])
    mv = sb("mv", [P, T, 2])
    bn_x = sb("bn_x", [P, 2 * CH, 6])
    mv_x = sb("mv_x", [P, CH, 2])
    small = sb("small", [P, 8, CH])
    ss = sb("ss", [P, T, 2 * H])
    hr = sb("hr", [P, T, 2 * H])
    hh = sb("hh", [P, T, 2 * H])
    ln_v = sb("ln_v", [P, T])
    ln_r = sb("ln_r", [P, T])
    ln_h = sb("ln_h", [P, T])
    ln_b = sb("ln_b", [P, T])
    max2 = probs[:, 0, 0:2 * HG * T].rearrange("p (n a) -> p n a", a=2)
    max1 = probs[:, 1, 0:HG * T]
    max_rows = probs[0:HG * T, 2, 0:P]
    logits_sb = sb("logits_sb", [P, T * E])
    score_ps = [ctx.enter_context(nc.psum_tensor(f"scores{i}", [P, HG * QB], F32)) for i in range(2)]
    acc_ps = [ctx.enter_context(nc.psum_tensor(f"acc{i}", [P, BANK], F32)) for i in range(2)]
    shared_ps = [ctx.enter_context(nc.psum_tensor(f"shared{i}", [P, BANK], F32)) for i in range(2)]
    sems = {}

    def sem(name):
        if name not in sems:
            sems[name] = ctx.enter_context(nc.semaphore(name))
        return sems[name]

    zero_rows = resid[MAX_ROW:P, 0:T // 2, :].rearrange("p t n -> p (t n)")
    one_row = resid[MAX_ROW:MAX_ROW + 1, T // 2:T, :].rearrange("p t n -> p (t n)")
    names = ("x_loaded group_copied0 group_copied1 v_copied0 v_copied1 max_row_in0 max_row_in1 tokens_out "
             "logits_out full0 full1 read0 read1 scores_ready exp_done weighed mean_ready dev_ready "
             "channel_r_ready xn_ready x_sum_ready squared squares_summed head_v_ready head_r_ready "
             "head_scaled last_heads_scaled dots_ready z_ready hi_ready moments_ready row_r_ready pool_done "
             "stats_ready x_stats_ready z2_ready maxima_ready resid_ready dve_done stack_rows summed "
             "blocks_done acc_copied norm_squared bound_ready shift_known attn_ready recip_ready").split()
    sems = {n: ctx.enter_context(nc.semaphore(n)) for n in names}
    nums = sorted(s.num for s in sems.values())
    assert nums == list(range(nums[0], nums[-1] + 1))
    env = dict(env)
    env.update(locals())

    with nc.Block() as block:
        @block.vector
        def _(dve):
            dve.memset(zero_rows, 0.0).then_inc(sems["stack_rows"], 1)
            dve.memset(one_row, 1.0).then_inc(sems["stack_rows"], 1)
            dve.tensor_scalar(head_ones[:, :], env["head_mask"][:, 0, :], float(N), None, ALU.mult) \
               .then_inc(sems["stack_rows"], 1)
            dve.wait_ge(sems["stack_rows"], 3)

    def ended():
        nc.all_engine_barrier()
        nc.gpsimd.sem_clear(range(nums[0], nums[-1] + 1))
        nc.all_engine_barrier()

    def attended(b, **work):
        needs_shift = nc.values_load(shifted[0:1, 0:1], min_val=0, max_val=1)
        with nc.If(needs_shift > 0):
            build_shift(nc, env)
            ended()
        build_batch(nc, env, b, attend=True, **work)
        ended()
        with nc.If(needs_shift > 0):
            with nc.Block() as block:
                @block.vector
                def _(dve):
                    dve.memset(query_stack[MAX_ROW:MAX_ROW + 1, :, :].bitcast(F32), 0.0) \
                       .then_inc(sems["stack_rows"], 1)
                    dve.wait_ge(sems["stack_rows"], 1)

                for engine in (block.sync, block.tensor, block.scalar, block.gpsimd):
                    @engine
                    def _(eng):
                        eng.wait_ge(sems["stack_rows"], 1)
            ended()

    ended()
    build_batch(nc, env, 0, front=True)
    ended()
    attended(0, front=True)
    with nc.Fori(1, B - 1) as b:
        attended(b, front=True, store=True)
    attended(B - 1, store=True)
    build_batch(nc, env, B, store=True)
    ended()


def copy_group(sp, env, g):
    hi, lo, query_stack, key_stack, s = (env[k] for k in ("hi", "lo", "query_stack", "key_stack", "sems"))
    for r in range(HG):
        h, src = HG * g + r, slice(DH * r, DH * (r + 1))
        for quarter, q_part, k_part in ((0, hi, hi), (1, hi, lo), (2, lo, hi)):
            dst = slice(DH * quarter, DH * (quarter + 1))
            sp.dma_start(query_stack[dst, h, :].bitcast(F32), q_part[src, 2 * g, :]) \
              .then_inc(s[f"group_copied{g}"], 16)
            sp.dma_start(key_stack[dst, h, :].bitcast(F32), k_part[src, 2 * g + 1, :]) \
              .then_inc(s[f"group_copied{g}"], 16)


STACK_DMAS = 6 * HG * 16


def build_shift(nc, env):
    s, ident = env["sems"], env["ident"]
    query_stack, key_stack, max2, max1, max_rows, shared_ps = (
        env[k] for k in ("query_stack", "key_stack", "max2", "max1", "max_rows", "shared_ps"))
    TILES = HG * T * 2
    USES = TILES + 1

    def full(eng, k):
        eng.wait_ge(s[f"full{k % 2}"], k // 2 + 1)
        return shared_ps[k % 2]

    with nc.Block() as block:
        @block.sync
        def _(sp):
            copy_group(sp, env, 1)
            for g in range(G):
                k = g * USES + TILES
                sp.wait_ge(s[f"read{k % 2}"], k // 2 + 1)
                sp.dma_start(query_stack[MAX_ROW:MAX_ROW + 1, HG * g:HG * (g + 1), :].bitcast(F32),
                             max_rows[:, :]).then_inc(s[f"max_row_in{g}"], 16)
                sp.wait_ge(s[f"max_row_in{g}"], 16)

        @block.tensor
        def _(pe):
            pe.wait_ge(s["group_copied1"], STACK_DMAS)
            for g in range(G):
                for n in range(USES):
                    k = g * USES + n
                    r, qt, kh = n // (2 * T), n // 2 % T, n % 2
                    if k >= 2:
                        pe.wait_ge(s[f"read{k % 2}"], k // 2)
                    if n < TILES:
                        last = pe.matmul(shared_ps[k % 2][:, :],
                                         query_stack[0:MAX_ROW, HG * g + r, P * qt:P * (qt + 1)],
                                         key_stack[0:MAX_ROW, HG * g + r, BANK * kh:BANK * (kh + 1)],
                                         start=True, stop=True)
                    else:
                        pe.wait_ge(s["maxima_ready"], g + 1)
                        last = pe.transpose(shared_ps[k % 2][0:HG * T, 0:P], max1[:, :], ident[:, :])
                    last.then_inc(s[f"full{k % 2}"], 1)

        @block.vector
        def _(dve):
            for g in range(G):
                for n in range(USES):
                    k = g * USES + n
                    if n < TILES:
                        ps = full(dve, k)
                        dve.tensor_reduce(max2[:, n // 2, n % 2:n % 2 + 1], ps[:, :], AX.X, ALU.max) \
                           .then_inc(s[f"read{k % 2}"], 1)
                        continue
                    for j in (k - 2, k - 1):
                        dve.wait_ge(s[f"read{j % 2}"], j // 2 + 1)
                    dve.tensor_reduce(max1[:, :], max2[:, :, :], AX.X, ALU.max).then_inc(s["maxima_ready"], 1)

        @block.scalar
        def _(act):
            for g in range(G):
                k = g * USES + TILES
                if g:
                    act.wait_ge(s["max_row_in0"], 16)
                ps = full(act, k)
                act.activation(max_rows.bitcast(F32R), ps[0:HG * T, 0:P], ACT.Copy, scale=-1.0) \
                   .then_inc(s[f"read{k % 2}"], 1)

        @block.gpsimd
        def _(pool):
            for g in range(G):
                pool.wait_ge(s[f"max_row_in{g}"], 16)


def build_batch(nc, env, b, front=False, attend=False, store=False):
    s = env["sems"]
    nxt = b + 1 if attend else b
    steps = order(attend, front, store)
    dealt = (UNITS if front else 4 * T) if attend else 1
    slots = spread(steps, dealt) + [[]] * (UNITS - dealt if attend else 0)
    use = bank_uses(slots)
    (key_stack, query_stack, hi, lo, v_sb, v_next, x_sb, chan, rows, lin_out, resid, attn_T, probs, squares,
     qT, z2T, qk0, dots_sb, sumv_sb, x_sum, bn6, bn_x, mv, mv_x, small, ss, hr, hh, ln_v, ln_r, ln_h, ln_b,
     prob_sum, acc_sb, head_ones, norm_sq, norm_max, bound, shifted, logits_sb, score_ps, acc_ps,
     shared_ps) = (env[k] for k in (
        "key_stack query_stack hi lo v_sb v_next x_sb chan rows lin_out resid attn_T probs squares "
        "qT z2T qk0 dots_sb sumv_sb x_sum bn6 bn_x mv mv_x small ss hr hh ln_v ln_r ln_h ln_b "
        "prob_sum acc_sb head_ones norm_sq norm_max bound shifted logits_sb score_ps acc_ps shared_ps").split())
    ident, ones, gn_mean, head_mask, w0_sb, w1T, waggT, bias, gate_w, gb = (env[k] for k in (
        "ident ones gn_mean head_mask w0_sb w1T waggT bias gate_w gb").split())
    squared_order = [x[1:] for x in steps if x[0] == "square"]
    direct = DIRECT if front else DIRECT_ALONE
    added = T - 1 - direct
    pool_quarters = 3 if attend else 2
    late = int(store)

    def bank(step):
        k = use[step]
        return shared_ps[k % 2], k % 2, k // 2

    def await_full(eng, *step):
        ps, i, nth = bank(step)
        eng.wait_ge(s[f"full{i}"], nth + 1)
        return ps

    def read(instruction, *step):
        instruction.then_inc(s[f"read{bank(step)[1]}"], 1)

    def await_read(eng, *step):
        _, i, nth = bank(step)
        eng.wait_ge(s[f"read{i}"], nth + 1)

    def scale_heads(eng, quarter):
        for t in range(T // 4 * quarter, T // 4 * (quarter + 1)):
            await_read(eng, "qk0", t)
            view = qk0[:, t, :].rearrange("p (h d) -> p h d", d=DH)
            last = eng.tensor_tensor(view, view, hr[:, t, :].unsqueeze(2).to_broadcast([P, 2 * H, DH]), ALU.mult)
        return last

    with nc.Block() as block:

        @block.sync
        def _(sp):
            waits = []

            def copy_v(g):
                sp.dma_start(v_sb[:, :, P * g:P * (g + 1)], v_next[:, :, P * g:P * (g + 1)]) \
                  .then_inc(s[f"v_copied{g}"], 16)
                waits.append((f"v_copied{g}", 16))

            if front and attend:
                sp.dma_start(x_sb[:, :, :], env["x_v"][nxt, :, :, :]).then_inc(s["x_loaded"], 16)
                waits.append(("x_loaded", 16))
            if front and not attend:
                for target, source in ((key_stack[MAX_ROW:MAX_ROW + 1], env["one_row"]),
                                       (key_stack[MAX_ROW + 1:P], env["zero_rows"][1:P - MAX_ROW]),
                                       (query_stack[MAX_ROW:P], env["zero_rows"])):
                    sp.dma_start(target.bitcast(F32), source.unsqueeze(1).to_broadcast([source.shape[0], H, N])) \
                      .then_inc(s["stack_rows"], 16)
                waits.append(("stack_rows", 48))
            if attend:
                copy_group(sp, env, 1)
                waits.append(("group_copied1", STACK_DMAS))
                copy_v(1)
            if store:
                for h in range(2):
                    part = slice(T // 2 * h, T // 2 * (h + 1))
                    await_read(sp, "agg", part.stop - 2)
                    await_read(sp, "agg", part.stop - 1)
                    sp.dma_start(env["out_v"][b - 1, :, part, :], resid[:, part, :]).then_inc(s["tokens_out"], 16)
                    sp.dma_start(env["tok_v"][b - 1, :, part, :], resid[:, part, :]).then_inc(s["tokens_out"], 16)
                waits.append(("tokens_out", 64))
                for t in range(T - 2, T):
                    await_read(sp, "gate", t)
                sp.dma_start(env["logits_d"][b - 1, :, :], logits_sb[:, :]).then_inc(s["logits_out"], 16)
                waits.append(("logits_out", 16))
            if front:
                if attend:
                    sp.wait_ge(s["weighed"], UNITS // 2)
                for h in range(2):
                    for j in range(2):
                        await_read(sp, "proj", j, h)
                copy_group(sp, env, 0)
                waits.append(("group_copied0", STACK_DMAS))
                await_read(sp, "v", T // 2 - 1)
                copy_v(0)
                sp.wait_ge(s["shift_known"], 1)
            for name, value in waits:
                sp.wait_ge(s[name], value)

        @block.tensor
        def _(pe):
            def scores(u):
                g, qb, kt = u // (NQB * T), u // T % NQB, u % T
                if u == UNITS // 2:
                    pe.wait_ge(s["group_copied1"], STACK_DMAS)
                if u >= 2:
                    pe.wait_ge(s["exp_done"], u - 1)
                for r in range(HG):
                    last = pe.matmul(score_ps[u % 2][:, QB * r:QB * (r + 1)],
                                     key_stack[:, HG * g + r, P * kt:P * (kt + 1)],
                                     query_stack[:, HG * g + r, QB * qb:QB * (qb + 1)], start=True, stop=True)
                last.then_inc(s["scores_ready"], 1)

            def weigh(u):
                g, blk, kt = u // (NQB * T), u // T, u % T
                if u == UNITS // 2:
                    pe.wait_ge(s["v_copied1"], 16)
                if kt == 0 and blk + late >= 2:
                    pe.wait_ge(s["acc_copied"], blk + late - 1)
                pe.wait_ge(s["exp_done"], u + 1)
                acc, p = acc_ps[blk % 2], probs[:, u % 3, :]
                for r in range(HG if kt > added else 0):
                    pe.matmul(acc[DH * r:DH * (r + 1), QB:2 * QB], ones[:, 0:DH], p[:, QB * r:QB * (r + 1)],
                              start=False, stop=False, skip_group_check=True, tile_position=(0, DH * r))
                for r in range(HG):
                    last = pe.matmul(acc[DH * r:DH * (r + 1), 0:QB],
                                     v_sb[:, kt, P * g + DH * r:P * g + DH * (r + 1)],
                                     p[:, QB * r:QB * (r + 1)], start=kt == 0, stop=kt == T - 1,
                                     skip_group_check=True, tile_position=(0, DH * r))
                last.then_inc(s["weighed"], 1)

            def total(blk):
                if blk >= 0:
                    pe.wait_ge(s["summed"], 2 * added * (blk + 1))
                for r in range(HG):
                    last = pe.matmul(acc_ps[blk % 2][DH * r:DH * (r + 1), QB:2 * QB], ones[:, 0:DH],
                                     prob_sum[:, blk % 2, QB * r:QB * (r + 1)], start=False, stop=True,
                                     skip_group_check=True, tile_position=(0, DH * r))
                last.then_inc(s["blocks_done"], 1)

            def transposes(ps, *blocks):
                for j, m in enumerate(blocks):
                    last = pe.transpose(ps[:, P * j:P * (j + 1)], m, ident[:, :])
                return last

            def product(out, pairs):
                for j, (stationary, moving) in enumerate(pairs):
                    last = pe.matmul(out, stationary, moving, start=j == 0, stop=j == len(pairs) - 1)
                return last

            def step(st):
                kind, *at = st
                if kind in BANKLESS:
                    return
                ps, i, nth = bank(st)
                if nth:
                    pe.wait_ge(s[f"read{i}"], nth)
                tok = [slice(P * t, P * (t + 1)) for t in range(T)]
                half = [slice(P * c, P * (c + 1)) for c in range(CH)]
                if kind == "agg":
                    if at[0] == T - QB // P:
                        pe.wait_ge(s["attn_ready"], late)
                    last = product(ps[:, 0:C], [(attn_T[:, c, tok[at[0]]], waggT[:, c, :]) for c in range(CH)])
                elif kind == "z2T":
                    pe.wait_ge(s["z2_ready"], at[0] + 1)
                    last = transposes(ps, *(rows[:, at[0], half[c]] for c in range(CH)))
                elif kind == "gate":
                    await_read(pe, "z2T", at[0])
                    last = product(ps[:, 0:E], [(z2T[:, c, tok[at[0]]], gate_w[:, c, :]) for c in range(CH)])
                elif kind == "xT":
                    c, h = at
                    if attend:
                        pe.wait_ge(s["x_loaded"], 16)
                    last = transposes(ps, *(x_sb[:, 4 * h + j, half[c]] for j in range(4)))
                elif kind == "gmean":
                    pe.wait_ge(s["mean_ready"], 1)
                    last = product(ps[:, 0:CH], [(gn_mean[:, :], small[:, 0, :])])
                elif kind == "gvar":
                    pe.wait_ge(s["dev_ready"], 1)
                    last = product(ps[:, 0:CH], [(gn_mean[:, :], small[:, 3, :])])
                elif kind == "qk0":
                    pe.wait_ge(s["xn_ready"], at[0] // (T // 2) + 1)
                    last = product(ps[:, :], [(chan[:, c, tok[at[0]]], w0_sb[:, c, 0:2 * C]) for c in range(CH)])
                elif kind == "v0":
                    last = product(ps[:, 0:C],
                                   [(chan[:, c, tok[at[0]]], w0_sb[:, c, 2 * C:3 * C]) for c in range(CH)])
                elif kind == "sumv":
                    pe.wait_ge(s["x_sum_ready"], 1)
                    last = product(ps[:, 0:C], [(x_sum[:, c, :], w0_sb[:, c, 2 * C:3 * C]) for c in range(CH)])
                elif kind == "dots":
                    pe.wait_ge(s["head_scaled"], pool_quarters)
                    pe.wait_ge(s["last_heads_scaled"], 4 - pool_quarters)
                    await_read(pe, "v0", T - 1)
                    for c in range(CH):
                        last = product(ps[:, half[c]], [(qk0[:, t, C + P * c:C + P * (c + 1)], rows[:, t, half[c]])
                                                        for t in range(T)])
                elif kind == "qT":
                    c, h = at
                    pe.wait_ge(s["head_scaled"], pool_quarters if h else 2)
                    if h:
                        pe.wait_ge(s["last_heads_scaled"], 4 - pool_quarters)
                    last = transposes(ps, *(qk0[:, 4 * h + j, half[c]] for j in range(4)))
                elif kind == "lin":
                    for c in range(CH):
                        await_read(pe, "qT", c, at[0] // 4)
                    pe.wait_ge(s["dots_ready"], 1)
                    for c in range(CH):
                        last = product(ps[:, half[c]], [(qT[:, c, tok[at[0]]], dots_sb[:, c, :])])
                elif kind == "zT":
                    c, h = at
                    pe.wait_ge(s["z_ready"], T // 2 * (h + 1))
                    last = transposes(ps, *(rows[:, 4 * h + j, half[c]] for j in range(4)))
                elif kind == "proj":
                    j, h = at
                    w = C * (j % 2) + P * (j // 2)
                    await_read(pe, "zT", CH - 2, h)
                    await_read(pe, "zT", CH - 1, h)
                    last = product(ps[:, :], [(w1T[:, c, w:w + P], chan[:, c, BANK * h:BANK * (h + 1)])
                                              for c in range(CH)])
                elif kind == "v":
                    for j in range(2):
                        last = product(ps[:, C * j:C * (j + 1)],
                                       [(chan[:, c, tok[2 * at[0] + j]], w1T[:, c, 2 * C:3 * C]) for c in range(CH)])
                elif kind == "norms":
                    n = squared_order.index(tuple(at))
                    pe.wait_ge(s["norm_squared"], n + 1)
                    last = product(ps[:, :], [(head_ones[:, :], norm_sq[:, :])])
                elif kind == "bound":
                    pe.wait_ge(s["bound_ready"], 1)
                    last = pe.transpose(ps[0:1, 0:P], bound[:, 0:1], ident[:, :])
                last.then_inc(s[f"full{i}"], 1)

            if attend:
                scores(0)
            for u, slot in enumerate(slots):
                if attend and u + 1 < UNITS:
                    scores(u + 1)
                if u == 0 and late:
                    total(-1)
                for st in slot[:1]:
                    step(st)
                if attend and u:
                    weigh(u - 1)
                for st in slot[1:]:
                    step(st)
                if attend and u > T and u % T == 1:
                    total(u // T - 1)
            if attend:
                weigh(UNITS - 1)

        @block.scalar
        def _(act):
            def layer_norm(src, t, before):
                act.wait_ge(s["row_r_ready"], before + t // (T // 2) + 1)
                return act.activation(rows[:, t, :], src[:, t, :], ACT.Identity,
                                      bias=ln_b[:, t:t + 1], scale=ln_r[:, t:t + 1])

            def step(st):
                kind, *at = st
                if kind == "store_rows":
                    layer_norm(resid, at[0], 0).then_inc(s["z2_ready"], 1)
                elif kind == "front_rows":
                    layer_norm(lin_out, at[0], 2 * late).then_inc(s["z_ready"], 1)
                if kind == "z2T":
                    ps = await_full(act, *st)
                    if at[0] == 0 and attend:
                        act.wait_ge(s["group_copied1"], STACK_DMAS)
                    read(act.activation(z2T[:, :, P * at[0]:P * (at[0] + 1)],
                                        ps[:, 0:C].rearrange("p (c n) -> p c n", c=CH), ACT.Copy), *st)
                elif kind in ("xT", "zT"):
                    c, h = at
                    ps = await_full(act, *st)
                    read(act.activation(chan[:, c, BANK * h:BANK * (h + 1)], ps[:, :], ACT.Copy), *st)
                elif kind == "qk0":
                    if at[0] == 0 and attend:
                        act.wait_ge(s["group_copied1"], STACK_DMAS)
                        act.wait_ge(s["v_copied1"], 16)
                    ps = await_full(act, *st)
                    read(act.activation(qk0[:, at[0], :], ps[:, :], ACT.Copy), *st)
                elif kind == "v0":
                    t = at[0]
                    await_read(act, "qk0", t)
                    if t >= 2:
                        act.wait_ge(s["squares_summed"], t - 1)
                    act.activation(squares[:, t % 2, :], qk0[:, t, :], ACT.Square).then_inc(s["squared"], 1)
                    ps = await_full(act, *st)
                    read(act.activation(rows[:, t, :], ps[:, 0:C], ACT.Copy), *st)
                elif kind == "qT":
                    c, h = at
                    ps = await_full(act, *st)
                    read(act.activation(qT[:, c, BANK * h:BANK * (h + 1)], ps[:, :], ACT.Identity,
                                        bias=gb[:, 1:2], scale=gb[:, 0:1]), *st)
                elif kind == "proj":
                    j, h = at
                    ps = await_full(act, *st)
                    act.activation(hi[:, j, BANK * h:BANK * (h + 1)].bitcast(F32R), ps[:, :], ACT.Copy) \
                       .then_inc(s["hi_ready"], 1)
                elif kind == "square":
                    j, h = at
                    n = squared_order.index(tuple(at))
                    act.wait_ge(s["hi_ready"], 4 * h + j + 1)
                    if n:
                        await_full(act, "norms", *squared_order[n - 1])
                    act.activation(norm_sq[:, :], hi[:, j, BANK * h:BANK * (h + 1)], ACT.Square) \
                       .then_inc(s["norm_squared"], 1)
                elif kind == "v":
                    ps = await_full(act, *st)
                    if at[0] == 0 and attend:
                        act.wait_ge(s["v_copied1"], 16)
                    read(act.activation(v_next[:, 2 * at[0]:2 * at[0] + 2, :],
                                        ps[:, :].rearrange("p (t n) -> p t n", t=2), ACT.Copy), *st)

            def copy_acc(blk):
                act.wait_ge(s["blocks_done"], blk + late + 1)
                if blk + late:
                    act.wait_ge(s["attn_ready"], blk + late)
                act.activation(acc_sb[:, :], acc_ps[blk % 2][:, :], ACT.Copy) \
                   .then_inc(s["acc_copied"], 1)

            for u, slot in enumerate(slots):
                if attend:
                    act.wait_ge(s["scores_ready"], u + 1)
                    if u >= 3:
                        act.wait_ge(s["weighed"], u - 2)
                        act.wait_ge(s["summed"], 2 * (added * ((u - 3) // T) + min(max((u - 3) % T, 1), added)))
                    act.activation(probs[:, u % 3, :], score_ps[u % 2][:, :], ACT.Exp, scale=DH ** -0.5) \
                       .then_inc(s["exp_done"], 1)
                if u == 0 and late:
                    copy_acc(-1)
                for st in slot:
                    step(st)
                if attend and u > T and u % T == 2:
                    copy_acc(u // T - 1)

        @block.gpsimd
        def _(pool):
            link = Chain(pool, s["pool_done"])

            def divide(blk):
                g, qb = blk % (G * NQB) // NQB, blk % NQB
                pool.wait_ge(s["recip_ready"], blk + late + 1)
                if blk == 0 and store:
                    for t in range(T - 2, T):
                        await_read(pool, "agg", t)
                pool.tensor_tensor(attn_T[:, g, QB * qb:QB * (qb + 1)], acc_sb[:, 0:QB],
                                   acc_sb[:, QB:2 * QB], ALU.mult).then_inc(s["attn_ready"], 1)

            def negative_product(out, a, b):
                link(pool.tensor_tensor(out, a, b, ALU.mult))
                link(pool.tensor_scalar(out, out, -1.0, None, ALU.mult))

            def row_deviations(h, n):
                part = slice(T // 2 * h, T // 2 * (h + 1))
                pool.wait_ge(s["moments_ready"], n + 1)
                link(pool.tensor_scalar(ln_v[:, part], mv[:, part, 1], LN_EPS, None, ALU.add))
                rsqrt(pool, link, ln_v[:, part], ln_r[:, part], ln_h[:, part])
                negative_product(ln_b[:, part], mv[:, part, 0], ln_r[:, part])
                pool.sem_inc(s["row_r_ready"], 1)

            def step(st):
                kind, *at = st
                if kind == "store_stats":
                    row_deviations(at[0], at[0])
                elif kind == "front_stats":
                    row_deviations(at[0], at[0] + 2 * late)
                elif kind == "gvar":
                    await_read(pool, "gvar")
                    rsqrt(pool, link, small[:, 4, :], small[:, 5, :], small[:, 6, :])
                    pool.sem_inc(s["channel_r_ready"], 1)
                elif kind == "resid":
                    if at[0] == 0 and store:
                        pool.wait_ge(s["tokens_out"], 64)
                        pool.wait_ge(s["z2_ready"], T)
                    pool.tensor_tensor(resid[:, at[0], :], lin_out[:, at[0], :], bias[:, :], ALU.add) \
                        .then_inc(s["resid_ready"], 1)
                elif kind == "head_stats":
                    pool.wait_ge(s["head_v_ready"], at[0] + 1)
                    part = slice(T // 2 * at[0], T // 2 * (at[0] + 1))
                    rsqrt(pool, link, *(m[:, part, :].rearrange("p t h -> p (t h)") for m in (ss, hr, hh)))
                    pool.sem_inc(s["head_r_ready"], 1)
                elif kind == "head_scale" and at[0] < pool_quarters:
                    scale_heads(pool, at[0]).then_inc(s["head_scaled"], 1)

            if late:
                divide(-1)
            for u, slot in enumerate(slots):
                for st in slot:
                    step(st)
                if attend and u > T and u % T == 4:
                    divide(u // T - 1)

        @block.vector
        def _(dve):
            link = Chain(dve, s["dve_done"])

            def statistics(src, t):
                dve.bn_stats(bn6[:, t, :], src[:, t, :]).then_inc(s["stats_ready"], 1)

            def add_tokens(st, target, source):
                kind, t = st
                ps = await_full(dve, *st)
                read(dve.tensor_tensor(target[:, t, :], ps[:, 0:C], source[:, t, :], ALU.add), *st)
                if t % (T // 2):
                    await_read(dve, kind, t - 1)
                    statistics(target, t - 1)

            def moments(kind, src, h, n):
                part = range(T // 2 * h, T // 2 * (h + 1))
                await_read(dve, kind, part.stop - 1)
                statistics(src, part.stop - 1)
                dve.wait_ge(s["stats_ready"], T // 2 * (n + 1))
                for t in part:
                    last = dve.bn_aggr(mv[:, t, :], bn6[:, t, :])
                last.then_inc(s["moments_ready"], 1)

            def step(st):
                kind, *at = st
                if kind == "agg":
                    add_tokens(st, resid, resid)
                elif kind == "store_stats":
                    moments("agg", resid, at[0], at[0])
                elif kind == "gate":
                    ps = await_full(dve, *st)
                    read(dve.tensor_scalar(logits_sb[:, E * at[0]:E * (at[0] + 1)], ps[:, 0:E], CLIP, None, ALU.max),
                         *st)
                elif kind == "xT":
                    c, h = at
                    await_read(dve, *st)
                    dve.bn_stats(bn_x[:, 2 * c + h, :], chan[:, c, BANK * h:BANK * (h + 1)]) \
                       .then_inc(s["x_stats_ready"], 1)
                elif kind == "x_stats":
                    dve.wait_ge(s["x_stats_ready"], 2 * CH)
                    for c in range(CH):
                        last = dve.bn_aggr(mv_x[:, c, :], bn_x[:, 2 * c:2 * c + 2, :].rearrange("p a b -> p (a b)"))
                    link(last)
                    dve.tensor_copy(small[:, 0, :], mv_x[:, :, 0]).then_inc(s["mean_ready"], 1)
                elif kind == "gmean":
                    ps = await_full(dve, *st)
                    read(dve.tensor_copy(small[:, 1, :], ps[:, 0:CH]), *st)
                    await_read(dve, *st)
                    link(dve.tensor_tensor(small[:, 2, :], small[:, 0, :], small[:, 1, :], ALU.subtract))
                    link(dve.tensor_tensor(small[:, 3, :], small[:, 2, :], small[:, 2, :], ALU.mult))
                    dve.tensor_tensor(small[:, 3, :], small[:, 3, :], mv_x[:, :, 1], ALU.add) \
                       .then_inc(s["dev_ready"], 1)
                elif kind == "gvar":
                    ps = await_full(dve, *st)
                    read(dve.tensor_scalar(small[:, 4, :], ps[:, 0:CH], LN_EPS, None, ALU.add), *st)
                elif kind == "xn":
                    dve.wait_ge(s["channel_r_ready"], 1)
                    part = slice(BANK * at[0], BANK * (at[0] + 1))
                    for c in range(CH):
                        last = dve.tensor_scalar(chan[:, c, part], chan[:, c, part], small[:, 1, c:c + 1],
                                                 small[:, 5, c:c + 1], ALU.subtract, ALU.mult)
                    last.then_inc(s["xn_ready"], 1)
                elif kind == "x_sum":
                    dve.wait_ge(s["channel_r_ready"], 1)
                    link(dve.scalar_tensor_tensor(out=small[:, 7, :], in0=small[:, 2, :], scalar=float(N),
                                                  in1=small[:, 5, :], op0=ALU.mult, op1=ALU.mult))
                    for c in range(CH):
                        last = dve.tensor_scalar(x_sum[:, c, :], ones[:, :], small[:, 7, c:c + 1], None, ALU.mult)
                    last.then_inc(s["x_sum_ready"], 1)
                elif kind == "v0":
                    t = at[0]
                    dve.wait_ge(s["squared"], t + 1)
                    dve.tensor_reduce(ss[:, t, :], squares[:, t % 2, :].rearrange("p (h d) -> p h d", d=DH),
                                      AX.X, ALU.add).then_inc(s["squares_summed"], 1)
                elif kind == "head_stats":
                    part = slice(T // 2 * at[0], T // 2 * (at[0] + 1))
                    dve.wait_ge(s["squares_summed"], part.stop)
                    flat = ss[:, part, :].rearrange("p t h -> p (t h)")
                    dve.tensor_scalar(flat, flat, 1.0 / DH, LN_EPS, ALU.mult, ALU.add).then_inc(s["head_v_ready"], 1)
                elif kind == "head_scale" and at[0] >= pool_quarters:
                    dve.wait_ge(s["head_r_ready"], 2)
                    scale_heads(dve, at[0]).then_inc(s["last_heads_scaled"], 1)
                elif kind == "sumv":
                    ps = await_full(dve, *st)
                    read(dve.tensor_scalar(sumv_sb[:, :], ps[:, 0:C], gb[:, 3:4], None, ALU.mult), *st)
                elif kind == "dots":
                    await_read(dve, "sumv")
                    ps = await_full(dve, *st)
                    flat = dots_sb[:, :, :].rearrange("p c n -> p (c n)")
                    read(dve.scalar_tensor_tensor(out=flat, in0=ps[:, 0:C], scalar=gb[:, 2:3], in1=sumv_sb[:, :],
                                                  op0=ALU.mult, op1=ALU.add), *st)
                    await_read(dve, *st)
                    dve.tensor_tensor(flat, flat, head_mask[:, :, :].rearrange("p c n -> p (c n)"), ALU.mult) \
                       .then_inc(s["dots_ready"], 1)
                elif kind == "lin":
                    if at[0] == 0 and attend:
                        dve.wait_ge(s["resid_ready"], T)
                    add_tokens(st, lin_out, x_sb)
                elif kind == "front_stats":
                    moments("lin", lin_out, at[0], at[0] + 2 * late)
                elif kind == "proj":
                    j, h = at
                    part = slice(BANK * h, BANK * (h + 1))
                    ps = await_full(dve, *st)
                    dve.wait_ge(s["hi_ready"], 4 * h + j + 1)
                    read(dve.tensor_tensor(lo[:, j, part].bitcast(F32R), ps[:, :], hi[:, j, part], ALU.subtract), *st)
                elif kind == "norms":
                    j, h = at
                    ps = await_full(dve, *st)
                    read(dve.tensor_reduce(norm_max[:, j, h:h + 1], ps[:, :], AX.X, ALU.max), *st)
                elif kind == "bound_rows":
                    for j, h in squared_order[-2:]:
                        await_read(dve, "norms", j, h)
                    link(dve.tensor_reduce(bound[:, 1:5], norm_max[:, :, :], AX.X, ALU.max))
                    for g in range(G):
                        link(dve.tensor_tensor(bound[:, 5 + g:6 + g], bound[:, 1 + 2 * g:2 + 2 * g],
                                               bound[:, 2 + 2 * g:3 + 2 * g], ALU.mult))
                    dve.tensor_tensor(bound[:, 0:1], bound[:, 5:6], bound[:, 6:7], ALU.max) \
                       .then_inc(s["bound_ready"], 1)
                elif kind == "bound":
                    ps = await_full(dve, *st)
                    read(dve.tensor_reduce(bound[0:1, 7:8], ps[0:1, 0:P], AX.X, ALU.max), *st)
                    await_read(dve, *st)
                    dve.tensor_scalar(shifted[:, :], bound[0:1, 7:8], 0.99 * DH * SAFE_SCORE ** 2, None,
                                      ALU.is_gt).then_inc(s["shift_known"], 1)

            def invert(blk):
                dve.wait_ge(s["acc_copied"], blk + late + 1)
                dve.reciprocal(acc_sb[:, QB:2 * QB], acc_sb[:, QB:2 * QB]).then_inc(s["recip_ready"], 1)

            def add_up(u):
                kt, total = u % T, prob_sum[:, u // T % 2, :]
                if not 1 <= kt <= added:
                    return
                dve.wait_ge(s["exp_done"], u + 1)
                if kt == 1 and u // T + late >= 2:
                    dve.wait_ge(s["blocks_done"], u // T + late - 1)
                for h in range(2):
                    part = slice(BANK * h, BANK * (h + 1))
                    if kt > 1:
                        dve.wait_ge(s["summed"], 2 * (added * (u // T) + kt - 2) + h + 1)
                    dve.tensor_tensor(total[:, part], probs[:, (u - 1) % 3, part] if kt == 1 else total[:, part],
                                      probs[:, u % 3, part], ALU.add).then_inc(s["summed"], 1)

            if late:
                invert(-1)
            for u, slot in enumerate(slots):
                if attend and u:
                    add_up(u - 1)
                for st in slot:
                    step(st)
                if attend and u > T and u % T == 3:
                    invert(u // T - 1)
            if attend:
                add_up(UNITS - 1)


def build_experts(nc, ctx, env):
    def sb(name, shape, dt=F32):
        return ctx.enter_context(nc.sbuf_tensor(name, shape, dt))

    def ps(name, shape):
        return ctx.enter_context(nc.psum_tensor(name, shape, F32))

    ident, ones = env["ident"], env["ones"]
    tokens, out_rows = env["tokens"], env["out_rows"]
    BE = B * E
    HALF = BE * T // 2
    DIVISION_STEPS = 6
    gates = sb("gates", [P, B, T, E])
    gates_t = sb("gates_t", [P, T // 2, 2, B, E])
    col = sb("col", [P, B, E])
    col_r = sb("col_r", [P, B, E])
    row = sb("row", [P, B * T])
    row_r = sb("row_r", [P, B * T])
    work = sb("work", [P, 2, N // 2])
    best = sb("best", [P, M])
    best_i = sb("best_i", [P, M], U32)
    best_f = sb("best_f", [P, M])
    flip = sb("flip", [P, P])
    lists = sb("lists", [P, 2, 2, BE])
    from_first = sb("from_first", [P, BE])
    chosen_f = sb("chosen_f", [P, BE])
    first_token = sb("first_token", [P, B], I32)
    first_token_f = sb("first_token_f", [P, B])
    slot_token = sb("slot_token", [P, E, B], U32)
    slot_gate = sb("slot_gate", [P, E, B])
    w_sb = sb("w_sb", [P, E, CH, C])
    picked = sb("picked", [P, PICKED, B, C])
    z = sb("z", [P, 2, B, C])
    zT = sb("zT3", [P, 2, CH, P])
    result = sb("result", [P, 2, B, C])
    bn6 = sb("bn6e", [P, B, 6])
    mv = sb("mve", [P, B, 2])
    ln_v, ln_r, ln_h = sb("ln_ve", [P, B]), sb("ln_re", [P, B]), sb("ln_he", [P, B])
    wide_ps = ps("wide_ps", [P, 2 * BANK])
    zT_ps = [ps(f"zT_ps{i}", [P, BANK]) for i in range(2)]
    y_ps = [ps(f"y_ps{i}", [P, BANK]) for i in range(2)]
    names = ("logits_in w_in dve_done sums_ready0 sums_ready1 divided0 divided1 flip_filled flip_ready listed "
             "flipped turned gates_copied lists_ready lists_turned iota_done indexed chosen stats_ready "
             "z_ready zT_ready zT_read y_ready result_ready").split()
    s = {n: ctx.enter_context(nc.semaphore(n + "_e")) for n in names}
    s["scattered"] = ctx.enter_context(nc.semaphore("scattered"))
    s["first_in"] = [ctx.enter_context(nc.semaphore(f"first_in{b}")) for b in range(B)]
    s["picked_in"] = [ctx.enter_context(nc.semaphore(f"picked_in{i}")) for i in range(PICKED)]

    def gather(pool, e, b):
        pool.indirect_dma_start(picked[:, e % PICKED, b, :], None, tokens[:, :],
                                bass.IndirectOffsetOnAxis(ap=slot_token[:, e, b:b + 1], axis=0)) \
            .then_inc(s["picked_in"][e % PICKED] if e else s["first_in"][b], 16)

    with nc.Block() as block:
        @block.sync
        def _(sp):
            sp.dma_start(gates[:, :, :, :].rearrange("p b t e -> p b (t e)"),
                         env["logits_d"].rearrange("b p n -> p b n")).then_inc(s["logits_in"], 16)
            sp.dma_start(w_sb[:, :, :, :], env["wexp"].rearrange("e (c p) o -> p e c o", p=P)).then_inc(s["w_in"], 16)
            sp.wait_ge(s["w_in"], 16)

        @block.tensor
        def _(pe):
            pe.wait_ge(s["logits_in"], 16)
            for it in range(SINKHORN_ITERS):
                for h in range(2):
                    if it:
                        pe.wait_ge(s[f"divided{h}"], DIVISION_STEPS * it)
                    pe.matmul(wide_ps[:, BANK * h:BANK * h + HALF], ones[:, :],
                              gates[:, B // 2 * h:B // 2 * (h + 1)].rearrange("p b t e -> p (b t e)"),
                              start=True, stop=True).then_inc(s[f"sums_ready{h}"], 1)
            for h in range(2):
                pe.wait_ge(s[f"divided{h}"], DIVISION_STEPS * SINKHORN_ITERS + 1)
            for t in range(T // 2):
                last = pe.transpose(y_ps[0][:, P * t:P * (t + 1)],
                                    gates_t[:, t, :, :, :].rearrange("p h b e -> p (h b e)"), ident[:, :])
            last.then_inc(s["turned"], 1)
            pe.wait_ge(s["lists_ready"], 2)
            pe.transpose(zT_ps[0][:, 0:P], best_f[:, :], ident[:, :])
            pe.transpose(zT_ps[1][:, 0:P], best[:, :], ident[:, :]).then_inc(s["lists_turned"], 1)
            pe.wait_ge(s["flip_ready"], 1)
            pe.wait_ge(s["listed"], 2)
            for n in range(2):
                last = pe.matmul(wide_ps[:, BE * n:BE * (n + 1)], flip[:, :], lists[:, n, 1, :], start=True, stop=True)
            last.then_inc(s["flipped"], 1)
            pe.wait_ge(s["chosen"], 1)
            pe.wait_ge(s["w_in"], 16)

            def turn(n):
                pe.wait_ge(s["z_ready"], n + 1)
                if n >= 2:
                    pe.wait_ge(s["zT_read"], n - 1)
                for c in range(CH):
                    last = pe.transpose(zT_ps[n % 2][:, P * c:P * (c + 1)], z[:, n // B % 2, n % B, P * c:P * (c + 1)],
                                        ident[:, :])
                last.then_inc(s["zT_ready"], 1)

            def multiply(n):
                pe.wait_ge(s["zT_read"], n + 1)
                if n >= 2:
                    pe.wait_ge(s["result_ready"], n - 1)
                for c in range(CH):
                    last = pe.matmul(y_ps[n % 2][:, 0:C], zT[:, n % 2, c, :], w_sb[:, n // B, c, :],
                                     start=c == 0, stop=c == CH - 1)
                last.then_inc(s["y_ready"], 1)

            turn(0)
            for n in range(E * B):
                if n + 1 < E * B:
                    turn(n + 1)
                multiply(n)

        @block.gpsimd
        def _(pool):
            pool.iota(first_token[:, :], pattern=[[N, B]], base=0, channel_multiplier=0).then_inc(s["iota_done"], 1)
            pool.memset(flip[:, :], 0.0).then_inc(s["flip_filled"], 1)
            pool.wait_ge(s["flip_filled"], 1)
            pool.affine_select(out=flip[:, :], in_=flip[:, :], compare_op=ALU.not_equal, fill=1.0,
                               base=1 - P, pattern=[[1, P]], channel_multiplier=1).then_inc(s["flip_ready"], 1)
            pool.wait_ge(s["chosen"], 1)
            for e in range(2):
                for b in range(B):
                    gather(pool, e, b)
            for e in range(E):
                if e + 2 < E:
                    if e:
                        pool.wait_ge(s["result_ready"], B * e)
                    for b in range(B):
                        gather(pool, e + 2, b)
                if e:
                    pool.wait_ge(s["scattered"], 16 * B * e)
                for b in range(B):
                    pool.wait_ge(s["result_ready"], B * e + b + 1)
                    pool.indirect_dma_start(out_rows[:, :],
                                            bass.IndirectOffsetOnAxis(ap=slot_token[:, e, b:b + 1], axis=0),
                                            result[:, e % 2, b, :], None).then_inc(s["scattered"], 16)
            pool.wait_ge(s["scattered"], 16 * B * E)

        @block.vector
        def _(dve):
            link = Chain(dve, s["dve_done"])
            done = [0, 0]

            def divide_step(h, instruction):
                instruction.then_inc(s[f"divided{h}"], 1)
                done[h] += 1

            def await_half(h):
                dve.wait_ge(s[f"divided{h}"], done[h])

            halves = [slice(B // 2 * h, B // 2 * (h + 1)) for h in range(2)]
            by_token = [gates[:, b].rearrange("p b t e -> p (b t) e") for b in halves]
            dve.wait_ge(s["logits_in"], 16)
            for it in range(SINKHORN_ITERS):
                for h, b in enumerate(halves):
                    dve.wait_ge(s[f"sums_ready{h}"], it + 1)
                    divide_step(h, dve.tensor_reduce(
                        col[:, b], wide_ps[:, BANK * h:BANK * h + HALF].rearrange("p (b t e) -> p b e t", b=B // 2, t=T),
                        AX.X, ALU.add))
                for h, b in enumerate(halves):
                    await_half(h)
                    divide_step(h, dve.reciprocal(col_r[:, b], col[:, b]))
                for h, b in enumerate(halves):
                    await_half(h)
                    divide_step(h, dve.tensor_tensor(gates[:, b], gates[:, b], col_r[:, b].unsqueeze(2)
                                                     .to_broadcast([P, B // 2, T, E]), ALU.mult))
                rows_of = [slice(B // 2 * T * h, B // 2 * T * (h + 1)) for h in range(2)]
                for h, r in enumerate(rows_of):
                    await_half(h)
                    divide_step(h, dve.tensor_reduce(row[:, r], by_token[h], AX.X, ALU.add))
                for h, r in enumerate(rows_of):
                    await_half(h)
                    divide_step(h, dve.reciprocal(row_r[:, r], row[:, r]))
                for h, r in enumerate(rows_of):
                    await_half(h)
                    if it < SINKHORN_ITERS - 1:
                        divide_step(h, dve.tensor_tensor(by_token[h], by_token[h], row_r[:, r].unsqueeze(2)
                                                         .to_broadcast([P, B // 2 * T, E]), ALU.mult))
                        continue
                    shares = row_r[:, r].rearrange("p (b t) -> p b t", b=B // 2)
                    for k in range(2):
                        tiles = slice(T // 2 * k, T // 2 * (k + 1))
                        divide_step(h, dve.tensor_tensor(
                            gates_t[:, :, k, halves[h], :].rearrange("p t b e -> p b t e"), gates[:, halves[h], tiles],
                            shares[:, :, tiles].unsqueeze(3).to_broadcast([P, B // 2, T // 2, E]), ALU.mult))
            assert done == [DIVISION_STEPS * SINKHORN_ITERS + 1] * 2
            dve.wait_ge(s["turned"], 1)
            link(dve.tensor_copy(work[:, 0, :], y_ps[0][:, :]))
            for r in range(M // 8):
                eight = slice(8 * r, 8 * (r + 1))
                src, dst = work[:, r % 2, :], work[:, (r + 1) % 2, :]
                link(dve.max(best[:, eight], src))
                if r == M // 8 - 1:
                    link(dve.max_index(best_i[:, eight], best[:, eight], src))
                else:
                    dve.max_index(best_i[:, eight], best[:, eight], src).then_inc(s["indexed"], 1)
                    link(dve.match_replace(dst, best[:, eight], src, -1.0))
            dve.wait_ge(s["indexed"], M // 8 - 1)
            dve.sem_inc(s["lists_ready"], 1)
            dve.tensor_copy(best_f[:, :], best_i[:, :]).then_inc(s["lists_ready"], 1)
            dve.wait_ge(s["iota_done"], 1)
            link(dve.tensor_copy(first_token_f[:, :], first_token[:, :]))
            dve.wait_ge(s["lists_turned"], 1)
            for n in range(2):
                dve.tensor_copy(lists[:, n, :, :].rearrange("p h n -> p (h n)"), zT_ps[n][:, 0:P]) \
                   .then_inc(s["listed"], 1)
            dve.wait_ge(s["listed"], 2)
            dve.wait_ge(s["flipped"], 1)
            token, gate = lists[:, 0, 0, :], lists[:, 1, 0, :]
            other_token, other_gate = wide_ps[:, 0:BE], wide_ps[:, BE:2 * BE]
            dve.tensor_tensor(slot_gate[:, :, :].rearrange("p e b -> p b e"), gate.rearrange("p (b e) -> p b e", b=B),
                              other_gate.rearrange("p (b e) -> p b e", b=B), ALU.max)
            dve.tensor_tensor(from_first[:, :], gate, other_gate, ALU.is_ge)
            link(dve.scalar_tensor_tensor(out=chosen_f[:, :], in0=token, scalar=-N / 2, in1=other_token,
                                          op0=ALU.add, op1=ALU.subtract))
            link(dve.tensor_tensor(chosen_f[:, :], chosen_f[:, :], from_first[:, :], ALU.mult))
            link(dve.scalar_tensor_tensor(out=chosen_f[:, :], in0=other_token, scalar=N / 2, in1=chosen_f[:, :],
                                          op0=ALU.add, op1=ALU.add))
            link(dve.tensor_tensor(slot_token[:, 0:E, :].rearrange("p e b -> p b e"),
                                   chosen_f[:, :].rearrange("p (b e) -> p b e", b=B),
                                   first_token_f[:, :].unsqueeze(2).to_broadcast([P, B, E]), ALU.add))
            dve.sem_inc(s["chosen"], 1)

            def normalise(e):
                if e:
                    dve.wait_ge(s["picked_in"][e % PICKED], 16 * B * -(-e // PICKED))
                for b in range(B):
                    if not e:
                        dve.wait_ge(s["first_in"][b], 16)
                    dve.bn_stats(bn6[:, b, :], picked[:, e % PICKED, b, :]).then_inc(s["stats_ready"], 1)
                for b in range(B):
                    dve.wait_ge(s["stats_ready"], B * e + b + 1)
                    last = dve.bn_aggr(mv[:, b, :], bn6[:, b, :])
                link(last)
                link(dve.tensor_scalar(ln_v[:, :], mv[:, :, 1], LN_EPS, None, ALU.add))
                newton_rsqrt(dve, link, ln_v[:, :], ln_r[:, :], ln_h[:, :])
                if e >= 2:
                    dve.wait_ge(s["zT_ready"], B * (e - 1))
                for b in range(B):
                    dve.tensor_scalar(z[:, e % 2, b, :], picked[:, e % PICKED, b, :], mv[:, b, 0:1], ln_r[:, b:b + 1],
                                      ALU.subtract, ALU.mult).then_inc(s["z_ready"], 1)

            normalise(0)
            for e in range(E):
                if e + 1 < E:
                    normalise(e + 1)
                if e >= 2:
                    dve.wait_ge(s["scattered"], 16 * B * (e - 1))
                for b in range(B):
                    n = B * e + b
                    dve.wait_ge(s["y_ready"], n + 1)
                    dve.scalar_tensor_tensor(out=result[:, e % 2, b, :], in0=y_ps[n % 2][:, 0:C],
                                             scalar=slot_gate[:, e, b:b + 1], in1=picked[:, e % PICKED, b, :],
                                             op0=ALU.mult, op1=ALU.add).then_inc(s["result_ready"], 1)

        @block.scalar
        def _(act):
            for n in range(E * B):
                act.wait_ge(s["zT_ready"], n + 1)
                if n >= 2:
                    act.wait_ge(s["y_ready"], n - 1)
                act.activation(zT[:, n % 2, :, :].rearrange("p c n -> p (c n)"), zT_ps[n % 2][:, 0:C], ACT.Copy) \
                   .then_inc(s["zT_read"], 1)


_INS = ['x', 'L0_conv_w_qkv', 'L0_conv_q_gamma', 'L0_conv_q_beta', 'L0_conv_k_gamma', 'L0_conv_k_beta',
        'L1_attn_w_qkv', 'L1_attn_w_agg', 'L1_attn_b_agg', 'L1_ffn_gate_weight', 'L1_ffn_experts']
_OUTS = [((8, 32, 32, 256), 'float32')]


def kernel(**inputs):
    import numpy as _np
    import concourse.bacc as _bacc
    from concourse import mybir as _mybir
    from concourse.bass_utils import run_bass_kernel_spmd as _run

    nc = _bacc.Bacc("TRN2", target_bir_lowering=False, num_devices=1)
    arrays, args = {}, []
    for name in _INS:
        a = _np.ascontiguousarray(inputs[name])
        arrays[f"in_{name}_dram"] = a
        args.append(nc.dram_tensor(f"in_{name}_dram", a.shape, _mybir.dt.from_np(a.dtype), kind="ExternalInput").ap())
    for i, (shape, dtype) in enumerate(_OUTS):
        dt = _mybir.dt.from_np(_np.dtype(dtype))
        args.append(nc.dram_tensor(f"out_{i}_dram", shape, dt, kind="ExternalOutput").ap())
    hybrid_kernel(nc, *args)
    r = _run(nc, [arrays], core_ids=[0])
    return r.results[0]["out_0_dram"]
```
